# Optimizing a Trainium2 kernel written in Bass

```python
import numpy as np
import jax
import jax.numpy as jnp

def _softmax(x, axis=-1):
    return jax.nn.softmax(x, axis=axis)
def _gelu(x):
    return jax.nn.gelu(x, approximate=True)
def _silu(x):
    return jax.nn.silu(x)
def _sigmoid(x):
    return jax.nn.sigmoid(x)
def _layernorm(x, axis=-1, eps=1e-5):
    m = jnp.mean(x, axis=axis, keepdims=True)
    v = jnp.var(x, axis=axis, keepdims=True)
    return (x - m) / jnp.sqrt(v + eps)
def _scatter_add(tgt, idx, src, axis=0):
    return tgt.at[idx].add(src)
def _segment_sum(src, seg, n):
    return jax.ops.segment_sum(src, seg, n)

kernel_name = 'mk_conv_preact_d4_conv_nchw192_6d5073'

def setup_inputs(seed: int = 0):
    np.random.seed(seed)
    _w = jnp.asarray
    def _rec_inputs():
        import jax
        import jax.numpy as jnp
        _gk = jax.random.key(seed)
        x = -0.0005058 + 1 * jax.random.normal(jax.random.fold_in(_gk, 1), (2, 192, 96, 96), jnp.float32)
        return x
    x = _rec_inputs()
    def _L0_conv_setup():
        import jax, jax.numpy as jnp
        import numpy as np
        B, CIN, CMID, H, W, K, PAD = (2, 192, 180, 96, 96, 3, 1)

        def conv1x1(x, w, b):
            return jnp.einsum('bchw,oc->bohw', x, w) + b[None, :, None, None]

        def deform_conv2d(x, offset, weight, bias, pad=PAD):
            Bx, C, Hx, Wx = x.shape
            Cout, Cin, Kk, _ = weight.shape
            KK = Kk * Kk
            G = offset.shape[1] // (2 * KK)
            Cg = C // G
            off = offset.reshape(Bx, G, KK, 2, Hx, Wx)
            hh = jnp.arange(Hx, dtype=x.dtype)
            ww = jnp.arange(Wx, dtype=x.dtype)
            kys = (jnp.arange(KK) // Kk).astype(x.dtype) - pad
            kxs = (jnp.arange(KK) % Kk).astype(x.dtype) - pad
            sy = off[:, :, :, 0] + kys[None, None, :, None, None] + hh[None, None, None, :, None]
            sx = off[:, :, :, 1] + kxs[None, None, :, None, None] + ww[None, None, None, None, :]
            y0f = jnp.floor(sy)
            x0f = jnp.floor(sx)
            dy = sy - y0f
            dx = sx - x0f
            y0 = y0f.astype(jnp.int32)
            x0 = x0f.astype(jnp.int32)
            xg = x.reshape(Bx, G, Cg, Hx * Wx)

            def gather(yi, xi, wgt):
                valid = (yi >= 0) & (yi < Hx) & (xi >= 0) & (xi < Wx)
                idx = jnp.clip(yi, 0, Hx - 1) * Wx + jnp.clip(xi, 0, Wx - 1)
                idx = idx.reshape(Bx, G, 1, KK * Hx * Wx)
                v = jnp.take_along_axis(xg, idx, axis=3)
                wv = (wgt * valid.astype(x.dtype)).reshape(Bx, G, 1, KK * Hx * Wx)
                return v * wv
            val = gather(y0, x0, (1 - dy) * (1 - dx)) + gather(y0, x0 + 1, (1 - dy) * dx) + gather(y0 + 1, x0, dy * (1 - dx)) + gather(y0 + 1, x0 + 1, dy * dx)
            patches = val.reshape(Bx, C, KK, Hx, Wx)
            out = jnp.einsum('bikhw,oik->bohw', patches, weight.reshape(Cout, Cin, KK))
            return out + bias[None, :, None, None]
        key = jax.random.key(seed)
        ks = jax.random.split(key, 14)
        s = 0.05
        return {'x': jax.random.normal(ks[0], (B, CIN, H, W), jnp.float32), 'w_reduce': jax.random.normal(ks[1], (CMID, CIN), jnp.float32) * s, 'b_reduce': jax.random.normal(ks[2], (CMID,), jnp.float32) * s, 'w_offset': jax.random.normal(ks[3], (2 * CMID, CMID), jnp.float32) * s, 'b_offset': jax.random.normal(ks[4], (2 * CMID,), jnp.float32) * s, 'w_dcnw': jax.random.normal(ks[5], (CMID, CMID, K, K), jnp.float32) * s, 'b_dcnw': jax.random.normal(ks[6], (CMID,), jnp.float32) * s, 'w_dcnh': jax.random.normal(ks[7], (CMID, CMID, K, K), jnp.float32) * s, 'b_dcnh': jax.random.normal(ks[8], (CMID,), jnp.float32) * s, 'w_expand': jax.random.normal(ks[9], (CIN, CMID), jnp.float32) * s, 'b_expand': jax.random.normal(ks[10], (CIN,), jnp.float32) * s, 'w_attn': jax.random.normal(ks[11], (2, CMID), jnp.float32) * s, 'b_attn': jax.random.normal(ks[12], (2,), jnp.float32) * s}
    _L0_conv_all = _L0_conv_setup()
    _L0_conv_in = {k: v for k, v in _L0_conv_all.items() if k in ('w_reduce', 'b_reduce', 'w_offset', 'b_offset', 'w_dcnw', 'b_dcnw', 'w_dcnh', 'b_dcnh', 'w_expand', 'b_expand', 'w_attn', 'b_attn', )}
    del _L0_conv_all

    def _L1_conv_setup():
        import jax, jax.numpy as jnp
        from jax import lax
        import numpy as np
        B, C, H, W = (16, 192, 128, 128)
        key = jax.random.key(seed)
        k1, k2, k3 = jax.random.split(key, 3)
        x = jax.random.normal(k1, (B, C, H, W), dtype=jnp.float32)
        fan_in = C
        bound = 1.0 / np.sqrt(fan_in)
        merge_w = jax.random.uniform(k2, (C, C, 1, 1), dtype=jnp.float32, minval=-bound, maxval=bound)
        merge_b = jax.random.uniform(k3, (C,), dtype=jnp.float32, minval=-bound, maxval=bound)
        return {'x': x, 'merge_w': merge_w, 'merge_b': merge_b}
    _L1_conv_all = _L1_conv_setup()
    _L1_conv_in = {k: v for k, v in _L1_conv_all.items() if k in ('merge_w', 'merge_b', )}
    del _L1_conv_all

    def _L2_conv_setup():
        import jax, jax.numpy as jnp
        import numpy as np
        LN_EPS = 1e-05
        NEG_INF = -1e+38

        def wkv_scan(w, u, k, v):
            Bdim, T, C = k.shape

            def step(carry, kv_t):
                p, q, o = carry
                kt, vt = kv_t
                no = jnp.maximum(o, u + kt)
                A = jnp.exp(o - no)
                Bw = jnp.exp(u + kt - no)
                y = (A * p + Bw * vt) / (A * q + Bw)
                no2 = jnp.maximum(w + o, kt)
                A2 = jnp.exp(w + o - no2)
                B2 = jnp.exp(kt - no2)
                return ((A2 * p + B2 * vt, A2 * q + B2, no2), y)
            init = (jnp.zeros((Bdim, C), k.dtype), jnp.zeros((Bdim, C), k.dtype), jnp.full((Bdim, C), NEG_INF, k.dtype))
            kT = jnp.moveaxis(k, 1, 0)
            vT = jnp.moveaxis(v, 1, 0)
            _, ys = jax.lax.scan(step, init, (kT, vT))
            return jnp.moveaxis(ys, 0, 1)
        key = jax.random.key(seed)
        ks = jax.random.split(key, 8)
        B, C, H, W = (16, 192, 56, 56)
        s = 0.02
        x = jax.random.normal(ks[0], (B, C, H, W), jnp.float32)
        Wk = jax.random.normal(ks[1], (C, C), jnp.float32) * s
        Wv = jax.random.normal(ks[2], (C, C), jnp.float32) * s
        Wr = jax.random.normal(ks[3], (C, C), jnp.float32) * s
        Wo = jax.random.normal(ks[4], (C, C), jnp.float32) * s
        ln_g = jnp.ones((C,), jnp.float32)
        ln_b = jnp.zeros((C,), jnp.float32)
        w_decay = -6.0 + 0.1 * jax.random.normal(ks[5], (C,), jnp.float32)
        u = 0.1 * jax.random.normal(ks[6], (C,), jnp.float32)
        return {'x': x, 'Wk': Wk, 'Wv': Wv, 'Wr': Wr, 'Wo': Wo, 'ln_g': ln_g, 'ln_b': ln_b, 'w_decay': w_decay, 'u': u}
    _L2_conv_all = _L2_conv_setup()
    _L2_conv_in = {k: v for k, v in _L2_conv_all.items() if k in ('Wk', 'Wv', 'Wr', 'Wo', 'ln_g', 'ln_b', 'w_decay', 'u', )}
    del _L2_conv_all

    def _L3_conv_setup():
        import jax, jax.numpy as jnp
        from jax import lax
        import numpy as np
        import math
        DIM = 192
        D_INNER = DIM * 2
        DT_RANK = math.ceil(DIM / 16)
        D_STATE = 16
        B, H, W = (4, 64, 64)
        KCONV = 4

        def _forward(x, W_in, conv_w, conv_b, W_x, W_dt, b_dt, A_log, D, W_out):
            Bb, C, Hh, Ww = x.shape
            L = Hh * Ww
            x_flat = x.reshape(Bb, C, L).transpose(0, 2, 1)
            xz = x_flat @ W_in.T
            x_in, z_gate = jnp.split(xz, 2, axis=-1)
            xt = x_in.transpose(0, 2, 1)
            xt_pad = jnp.pad(xt, ((0, 0), (0, 0), (KCONV - 1, 0)))
            xc = lax.conv_general_dilated(xt_pad, conv_w, window_strides=(1,), padding='VALID', feature_group_count=D_INNER) + conv_b[None, :, None]
            x_conv = jax.nn.silu(xc)
            x_dbl = jnp.einsum('bdl,kd->blk', x_conv, W_x)
            dt, B_ssm, C_ssm = jnp.split(x_dbl, [DT_RANK, DT_RANK + D_STATE], axis=-1)
            dt_lin = dt @ W_dt.T + b_dt
            delta = jax.nn.softplus(dt_lin + b_dt)
            A = -jnp.exp(A_log)

            def step(h, inp):
                u_t, d_t, B_t, C_t = inp
                dA = jnp.exp(d_t[..., None] * A)
                h = dA * h + (d_t * u_t)[..., None] * B_t[:, None, :]
                y_t = jnp.einsum('bdn,bn->bd', h, C_t)
                return (h, y_t)
            u_seq = x_conv.transpose(2, 0, 1)
            d_seq = delta.transpose(1, 0, 2)
            B_seq = B_ssm.transpose(1, 0, 2)
            C_seq = C_ssm.transpose(1, 0, 2)
            h0 = jnp.zeros((Bb, D_INNER, D_STATE), x.dtype)
            _, ys = lax.scan(step, h0, (u_seq, d_seq, B_seq, C_seq))
            y = ys.transpose(1, 2, 0) + D[None, :, None] * x_conv
            y = y * jax.nn.silu(z_gate.transpose(0, 2, 1))
            out = jnp.einsum('bdl,cd->bcl', y, W_out)
            return out.reshape(Bb, C, Hh, Ww)
        key = jax.random.key(seed)
        ks = jax.random.split(key, 8)
        s = lambda k, shape, fan: jax.random.normal(k, shape, jnp.float32) / np.sqrt(fan).astype(np.float32)
        return {'x': jax.random.normal(ks[0], (B, DIM, H, W), jnp.float32), 'W_in': s(ks[1], (2 * D_INNER, DIM), DIM), 'conv_w': s(ks[2], (D_INNER, 1, KCONV), KCONV), 'conv_b': jnp.zeros((D_INNER,), jnp.float32), 'W_x': s(ks[3], (DT_RANK + 2 * D_STATE, D_INNER), D_INNER), 'W_dt': s(ks[4], (D_INNER, DT_RANK), DT_RANK), 'b_dt': jax.random.uniform(ks[5], (D_INNER,), jnp.float32, -4.0, -2.0), 'A_log': jnp.tile(jnp.log(jnp.arange(1, D_STATE + 1, dtype=jnp.float32)), (D_INNER, 1)), 'D': jnp.ones((D_INNER,), jnp.float32), 'W_out': s(ks[6], (DIM, D_INNER), D_INNER)}
    _L3_conv_all = _L3_conv_setup()
    _L3_conv_in = {k: v for k, v in _L3_conv_all.items() if k in ('W_in', 'conv_w', 'conv_b', 'W_x', 'W_dt', 'b_dt', 'A_log', 'D', 'W_out', )}
    del _L3_conv_all

    return {
        "x": x,
        "L0_conv_w_reduce": _L0_conv_in["w_reduce"],
        "L0_conv_b_reduce": _L0_conv_in["b_reduce"],
        "L0_conv_w_offset": _L0_conv_in["w_offset"],
        "L0_conv_b_offset": _L0_conv_in["b_offset"],
        "L0_conv_w_dcnw": _L0_conv_in["w_dcnw"],
        "L0_conv_b_dcnw": _L0_conv_in["b_dcnw"],
        "L0_conv_w_dcnh": _L0_conv_in["w_dcnh"],
        "L0_conv_b_dcnh": _L0_conv_in["b_dcnh"],
        "L0_conv_w_expand": _L0_conv_in["w_expand"],
        "L0_conv_b_expand": _L0_conv_in["b_expand"],
        "L0_conv_w_attn": _L0_conv_in["w_attn"],
        "L0_conv_b_attn": _L0_conv_in["b_attn"],
        "L1_conv_merge_w": _L1_conv_in["merge_w"],
        "L1_conv_merge_b": _L1_conv_in["merge_b"],
        "L2_conv_Wk": _L2_conv_in["Wk"],
        "L2_conv_Wv": _L2_conv_in["Wv"],
        "L2_conv_Wr": _L2_conv_in["Wr"],
        "L2_conv_Wo": _L2_conv_in["Wo"],
        "L2_conv_ln_g": _L2_conv_in["ln_g"],
        "L2_conv_ln_b": _L2_conv_in["ln_b"],
        "L2_conv_w_decay": _L2_conv_in["w_decay"],
        "L2_conv_u": _L2_conv_in["u"],
        "L3_conv_W_in": _L3_conv_in["W_in"],
        "L3_conv_conv_w": _L3_conv_in["conv_w"],
        "L3_conv_conv_b": _L3_conv_in["conv_b"],
        "L3_conv_W_x": _L3_conv_in["W_x"],
        "L3_conv_W_dt": _L3_conv_in["W_dt"],
        "L3_conv_b_dt": _L3_conv_in["b_dt"],
        "L3_conv_A_log": _L3_conv_in["A_log"],
        "L3_conv_D": _L3_conv_in["D"],
        "L3_conv_W_out": _L3_conv_in["W_out"],
    }

def reference(x, L0_conv_w_reduce, L0_conv_b_reduce, L0_conv_w_offset, L0_conv_b_offset, L0_conv_w_dcnw, L0_conv_b_dcnw, L0_conv_w_dcnh, L0_conv_b_dcnh, L0_conv_w_expand, L0_conv_b_expand, L0_conv_w_attn, L0_conv_b_attn, L1_conv_merge_w, L1_conv_merge_b, L2_conv_Wk, L2_conv_Wv, L2_conv_Wr, L2_conv_Wo, L2_conv_ln_g, L2_conv_ln_b, L2_conv_w_decay, L2_conv_u, L3_conv_W_in, L3_conv_conv_w, L3_conv_conv_b, L3_conv_W_x, L3_conv_W_dt, L3_conv_b_dt, L3_conv_A_log, L3_conv_D, L3_conv_W_out):
    import jax
    import jax.numpy as jnp
    def _L0_conv_ref(x, w_reduce, b_reduce, w_offset, b_offset, w_dcnw, b_dcnw, w_dcnh, b_dcnh, w_expand, b_expand, w_attn, b_attn):
        import jax, jax.numpy as jnp
        import numpy as np
        B, CIN, CMID, H, W, K, PAD = (2, 192, 180, 96, 96, 3, 1)

        def conv1x1(x, w, b):
            return jnp.einsum('bchw,oc->bohw', x, w) + b[None, :, None, None]

        def deform_conv2d(x, offset, weight, bias, pad=PAD):
            Bx, C, Hx, Wx = x.shape
            Cout, Cin, Kk, _ = weight.shape
            KK = Kk * Kk
            G = offset.shape[1] // (2 * KK)
            Cg = C // G
            off = offset.reshape(Bx, G, KK, 2, Hx, Wx)
            hh = jnp.arange(Hx, dtype=x.dtype)
            ww = jnp.arange(Wx, dtype=x.dtype)
            kys = (jnp.arange(KK) // Kk).astype(x.dtype) - pad
            kxs = (jnp.arange(KK) % Kk).astype(x.dtype) - pad
            sy = off[:, :, :, 0] + kys[None, None, :, None, None] + hh[None, None, None, :, None]
            sx = off[:, :, :, 1] + kxs[None, None, :, None, None] + ww[None, None, None, None, :]
            y0f = jnp.floor(sy)
            x0f = jnp.floor(sx)
            dy = sy - y0f
            dx = sx - x0f
            y0 = y0f.astype(jnp.int32)
            x0 = x0f.astype(jnp.int32)
            xg = x.reshape(Bx, G, Cg, Hx * Wx)

            def gather(yi, xi, wgt):
                valid = (yi >= 0) & (yi < Hx) & (xi >= 0) & (xi < Wx)
                idx = jnp.clip(yi, 0, Hx - 1) * Wx + jnp.clip(xi, 0, Wx - 1)
                idx = idx.reshape(Bx, G, 1, KK * Hx * Wx)
                v = jnp.take_along_axis(xg, idx, axis=3)
                wv = (wgt * valid.astype(x.dtype)).reshape(Bx, G, 1, KK * Hx * Wx)
                return v * wv
            val = gather(y0, x0, (1 - dy) * (1 - dx)) + gather(y0, x0 + 1, (1 - dy) * dx) + gather(y0 + 1, x0, dy * (1 - dx)) + gather(y0 + 1, x0 + 1, dy * dx)
            patches = val.reshape(Bx, C, KK, Hx, Wx)
            out = jnp.einsum('bikhw,oik->bohw', patches, weight.reshape(Cout, Cin, KK))
            return out + bias[None, :, None, None]
        xr = conv1x1(x, w_reduce, b_reduce)
        offs = conv1x1(xr, w_offset, b_offset)
        cm = xr.shape[1]
        off_w, off_h = (offs[:, :cm], offs[:, cm:])
        f_w = deform_conv2d(xr, off_w, w_dcnw, b_dcnw)
        f_h = deform_conv2d(xr, off_h, w_dcnh, b_dcnh)
        f_avg = (f_w + f_h).mean(axis=(2, 3), keepdims=True)
        attn = jax.nn.softmax(conv1x1(f_avg, w_attn, b_attn), axis=1)
        f_dcm = attn[:, 0:1] * f_h + attn[:, 1:2] * f_w
        return conv1x1(f_dcm, w_expand, b_expand)

    def _L1_conv_ref(x, merge_w, merge_b):
        import jax, jax.numpy as jnp
        from jax import lax
        import numpy as np
        B, C, H, W = (16, 192, 128, 128)
        c = x.shape[1]
        dn = lax.conv_dimension_numbers(x.shape, (c, 1, 3, 3), ('NCHW', 'OIHW', 'NCHW'))
        lap = jnp.array([[0.0, -1.0, 0.0], [-1.0, 4.0, -1.0], [0.0, -1.0, 0.0]], dtype=x.dtype)
        lap_k = jnp.broadcast_to(lap.reshape(1, 1, 3, 3), (c, 1, 3, 3))
        edges = lax.conv_general_dilated(x, lap_k, window_strides=(1, 1), padding=((1, 1), (1, 1)), dimension_numbers=dn, feature_group_count=c)
        out = x + edges
        dn1 = lax.conv_dimension_numbers(out.shape, merge_w.shape, ('NCHW', 'OIHW', 'NCHW'))
        y = lax.conv_general_dilated(out, merge_w, window_strides=(1, 1), padding='VALID', dimension_numbers=dn1)
        return y + merge_b[None, :, None, None]

    def _L2_conv_ref(x, Wk, Wv, Wr, Wo, ln_g, ln_b, w_decay, u):
        import jax, jax.numpy as jnp
        import numpy as np
        LN_EPS = 1e-05
        NEG_INF = -1e+38

        def wkv_scan(w, u, k, v):
            Bdim, T, C = k.shape

            def step(carry, kv_t):
                p, q, o = carry
                kt, vt = kv_t
                no = jnp.maximum(o, u + kt)
                A = jnp.exp(o - no)
                Bw = jnp.exp(u + kt - no)
                y = (A * p + Bw * vt) / (A * q + Bw)
                no2 = jnp.maximum(w + o, kt)
                A2 = jnp.exp(w + o - no2)
                B2 = jnp.exp(kt - no2)
                return ((A2 * p + B2 * vt, A2 * q + B2, no2), y)
            init = (jnp.zeros((Bdim, C), k.dtype), jnp.zeros((Bdim, C), k.dtype), jnp.full((Bdim, C), NEG_INF, k.dtype))
            kT = jnp.moveaxis(k, 1, 0)
            vT = jnp.moveaxis(v, 1, 0)
            _, ys = jax.lax.scan(step, init, (kT, vT))
            return jnp.moveaxis(ys, 0, 1)
        B, C, H, W = x.shape
        xs = jnp.transpose(x.reshape(B, C, H * W), (0, 2, 1))
        k = jnp.einsum('btc,dc->btd', xs, Wk)
        v = jnp.einsum('btc,dc->btd', xs, Wv)
        r = jnp.einsum('btc,dc->btd', xs, Wr)
        real_w = -jnp.exp(w_decay)
        x_fwd = wkv_scan(real_w, u, k, v)
        x_bwd = jnp.flip(wkv_scan(real_w, u, jnp.flip(k, 1), jnp.flip(v, 1)), 1)
        x_bi = 0.5 * (x_fwd + x_bwd)
        h = jax.nn.sigmoid(r) * x_bi
        mu = jnp.mean(h, axis=-1, keepdims=True)
        var = jnp.var(h, axis=-1, keepdims=True)
        h = (h - mu) * jax.lax.rsqrt(var + LN_EPS) * ln_g + ln_b
        out = jnp.einsum('btc,dc->btd', h, Wo)
        return jnp.transpose(out, (0, 2, 1)).reshape(B, C, H, W)

    def _L3_conv_ref(x, W_in, conv_w, conv_b, W_x, W_dt, b_dt, A_log, D, W_out):
        import jax, jax.numpy as jnp
        from jax import lax
        import numpy as np
        import math
        DIM = 192
        D_INNER = DIM * 2
        DT_RANK = math.ceil(DIM / 16)
        D_STATE = 16
        B, H, W = (4, 64, 64)
        KCONV = 4

        def _forward(x, W_in, conv_w, conv_b, W_x, W_dt, b_dt, A_log, D, W_out):
            Bb, C, Hh, Ww = x.shape
            L = Hh * Ww
            x_flat = x.reshape(Bb, C, L).transpose(0, 2, 1)
            xz = x_flat @ W_in.T
            x_in, z_gate = jnp.split(xz, 2, axis=-1)
            xt = x_in.transpose(0, 2, 1)
            xt_pad = jnp.pad(xt, ((0, 0), (0, 0), (KCONV - 1, 0)))
            xc = lax.conv_general_dilated(xt_pad, conv_w, window_strides=(1,), padding='VALID', feature_group_count=D_INNER) + conv_b[None, :, None]
            x_conv = jax.nn.silu(xc)
            x_dbl = jnp.einsum('bdl,kd->blk', x_conv, W_x)
            dt, B_ssm, C_ssm = jnp.split(x_dbl, [DT_RANK, DT_RANK + D_STATE], axis=-1)
            dt_lin = dt @ W_dt.T + b_dt
            delta = jax.nn.softplus(dt_lin + b_dt)
            A = -jnp.exp(A_log)

            def step(h, inp):
                u_t, d_t, B_t, C_t = inp
                dA = jnp.exp(d_t[..., None] * A)
                h = dA * h + (d_t * u_t)[..., None] * B_t[:, None, :]
                y_t = jnp.einsum('bdn,bn->bd', h, C_t)
                return (h, y_t)
            u_seq = x_conv.transpose(2, 0, 1)
            d_seq = delta.transpose(1, 0, 2)
            B_seq = B_ssm.transpose(1, 0, 2)
            C_seq = C_ssm.transpose(1, 0, 2)
            h0 = jnp.zeros((Bb, D_INNER, D_STATE), x.dtype)
            _, ys = lax.scan(step, h0, (u_seq, d_seq, B_seq, C_seq))
            y = ys.transpose(1, 2, 0) + D[None, :, None] * x_conv
            y = y * jax.nn.silu(z_gate.transpose(0, 2, 1))
            out = jnp.einsum('bdl,cd->bcl', y, W_out)
            return out.reshape(Bb, C, Hh, Ww)
        return _forward(x, W_in, conv_w, conv_b, W_x, W_dt, b_dt, A_log, D, W_out)

    def _gn(v, G=32, eps=1e-5):
        B_, C_, H_, W_ = v.shape
        g = v.reshape(B_, G, C_ // G, H_, W_)
        m = jnp.mean(g, axis=(2, 3, 4), keepdims=True)
        s = jnp.var(g, axis=(2, 3, 4), keepdims=True)
        return ((g - m) / jnp.sqrt(s + eps)).reshape(v.shape)

    def _ln_c(v, eps=1e-6):
        m = jnp.mean(v, axis=1, keepdims=True)
        s = jnp.var(v, axis=1, keepdims=True)
        return (v - m) / jnp.sqrt(s + eps)

    def _ln_t(v, eps=1e-5):
        m = jnp.mean(v, axis=-1, keepdims=True)
        s = jnp.var(v, axis=-1, keepdims=True)
        return (v - m) / jnp.sqrt(s + eps)

    def _to_tokens(v):
        B_, C_, H_, W_ = v.shape
        return v.reshape(B_, C_, H_ * W_).transpose(0, 2, 1)
    def _from_tokens(t, like):
        B_, C_, H_, W_ = like.shape
        return t.transpose(0, 2, 1).reshape(B_, C_, H_, W_)

    x = x + _L0_conv_ref(_gn(x), L0_conv_w_reduce, L0_conv_b_reduce, L0_conv_w_offset, L0_conv_b_offset, L0_conv_w_dcnw, L0_conv_b_dcnw, L0_conv_w_dcnh, L0_conv_b_dcnh, L0_conv_w_expand, L0_conv_b_expand, L0_conv_w_attn, L0_conv_b_attn)
    x = x + _L1_conv_ref(_gn(x), L1_conv_merge_w, L1_conv_merge_b)
    x = x + _L2_conv_ref(_gn(x), L2_conv_Wk, L2_conv_Wv, L2_conv_Wr, L2_conv_Wo, L2_conv_ln_g, L2_conv_ln_b, L2_conv_w_decay, L2_conv_u)
    x = x + _L3_conv_ref(_gn(x), L3_conv_W_in, L3_conv_conv_w, L3_conv_conv_b, L3_conv_W_x, L3_conv_W_dt, L3_conv_b_dt, L3_conv_A_log, L3_conv_D, L3_conv_W_out)
    return x


_drawn_inputs = setup_inputs


def setup_inputs(seed=0):
    import zlib

    import numpy as np

    out = dict(_drawn_inputs(seed))
    spreads = {'L2_conv_ln_g': (1.0, 0.6),
     'L2_conv_ln_b': (0.0, 0.8),
     'L3_conv_conv_b': (0.0, 0.641),
     'L3_conv_D': (1.0, 0.6)}
    factors = {'L0_conv_b_dcnh': 3.926,
     'L0_conv_w_attn': 3.278,
     'L0_conv_b_attn': 8.0,
     'L2_conv_Wr': 5.191,
     'L2_conv_w_decay': 8.0,
     'L2_conv_u': 28.9,
     'L3_conv_W_x': 4.715,
     'L3_conv_W_dt': 8.0,
     'L3_conv_b_dt': 8.0,
     'L3_conv_A_log': 8.0}
    for name, (base, spread) in spreads.items():
        noise = np.random.default_rng([zlib.crc32(name.encode()), seed]).standard_normal(out[name].shape)
        drawn = base * np.exp(spread * noise) if base else spread * noise
        out[name] = jnp.asarray(drawn.astype(out[name].dtype))
    for name, factor in factors.items():
        out[name] = (out[name] * factor).astype(out[name].dtype)
    return out
```

```python
import numpy as np
import concourse.bass as bass
from concourse import mybir
from concourse.alu_op_type import AluOpType as ALU
from contextlib import ExitStack

F32 = mybir.dt.float32
I32 = mybir.dt.int32
ACT = mybir.ActivationFunctionType
AX = mybir.AxisListType
DS = bass.DynSlice

B, C, CM, H, W = 2, 192, 180, 96, 96
HW = H * W
NG, TAPS, CG = 10, 9, 18
WIN = 7
NWIN = 14
FAR = 3.0
PADT = 4
ROWS = 200
EPS = 1e-5
NEAR1 = 2.0 ** -7
HC = C // 2
HM = CM // 2


def take(eng, sem, n=1):
    eng.wait_ge(sem, n).then_inc(sem, -n)


class Phase:

    def __init__(self, nc, name):
        self.nc, self.name, self.ctx, self.n = nc, name, ExitStack(), 0
        self.cell, self.turn = None, 0

    def __enter__(self):
        self.ctx.__enter__()
        return self

    def __exit__(self, *a):
        return self.ctx.__exit__(*a)

    def _name(self, kind):
        self.n += 1
        return f"{self.name}_{kind}{self.n}"

    def sb(self, shape, dt=F32):
        return self.ctx.enter_context(self.nc.sbuf_tensor(self._name("t"), shape, dt))

    def ps(self, shape):
        return self.ctx.enter_context(self.nc.psum_tensor(self._name("p"), shape, F32))

    def sem(self):
        return self.ctx.enter_context(self.nc.semaphore(self._name("s")))

    def sems(self, n):
        return [self.sem() for _ in range(n)]

    def tick(self, eng, sem):
        if self.cell is None:
            self.cell = self.sb([1, 16])
        self.turn = (self.turn + 1) % 16
        eng.memset(self.cell[:, self.turn:self.turn + 1], 0.0).then_inc(sem, 1)

    def block(self):
        return self.nc.Block()


class Shared:

    def __init__(self, tensors):
        self.d, self.n = dict(tensors), 0

    def fresh(self, name):
        self.n += 1
        return f"{name}{self.n}"


def group_norm_terms(nc, k, ST, nseg, GN):
    with Phase(nc, k.fresh("gn")) as p:
        MV = p.sb([HC, 4, 2])
        MG = p.sb([HC, 4])
        D = p.sb([HC, 4])
        Q = p.sb([HC, 4])
        V = p.sb([HC, 4])
        PM = p.ps([HC, 512])
        PV = p.ps([HC, 512])
        s_v, s_mv, s_m, s_q, s_var, s_e, s_sd = p.sems(7)
        with p.block() as blk:
            @blk.vector
            def _(e):
                for i in range(4):
                    ins = e.bn_aggr(MV[:, i, :], ST[:, i, 0:nseg, :])
                ins.then_inc(s_mv, 1)
                take(e, s_m)
                e.tensor_copy(MG[:, :], PM[:, 0:4]).then_inc(s_v, 1)
                take(e, s_v)
                e.tensor_tensor(D[:, :], MV[:, :, 0], MG[:, :], ALU.subtract).then_inc(s_v, 1)
                take(e, s_v)
                e.tensor_tensor(D[:, :], D[:, :], D[:, :], ALU.mult).then_inc(s_v, 1)
                take(e, s_v)
                e.tensor_tensor(Q[:, :], D[:, :], MV[:, :, 1], ALU.add).then_inc(s_q, 1)
                take(e, s_var)
                e.tensor_scalar(V[:, :], PV[:, 0:4], EPS, None, ALU.add).then_inc(s_e, 1)
                take(e, s_sd)
                e.reciprocal(GN[:, :, 0], V[:, :]).then_inc(s_v, 1)
                take(e, s_v)
                e.scalar_tensor_tensor(out=GN[:, :, 1], in0=MG[:, :], scalar=-1.0, in1=GN[:, :, 0],
                                       op0=ALU.mult, op1=ALU.mult)

            @blk.tensor
            def _(e):
                take(e, s_mv)
                e.matmul(PM[:, 0:4], k.G6[:, :], MV[:, :, 0], start=True, stop=True).then_inc(s_m, 1)
                take(e, s_q)
                e.matmul(PV[:, 0:4], k.G6[:, :], Q[:, :], start=True, stop=True).then_inc(s_var, 1)

            @blk.scalar
            def _(e):
                take(e, s_e)
                e.activation(V[:, :], V[:, :], ACT.Sqrt).then_inc(s_sd, 1)


def load_constants(nc, k):
    with Phase(nc, "cst") as p:
        s = p.sem()
        with p.block() as blk:
            @blk.sync
            def _(e):
                n = 0
                for dst, src in k.const_loads:
                    e.dma_start(dst, src).then_inc(s, 16)
                    n += 16
                e.wait_ge(s, n).then_inc(s, -n)


def first_norm_and_projections(nc, k):
    RC = 4
    NP = RC * W
    NCH = H // RC
    with Phase(nc, "in") as p:
        X = p.sb([HC, 4, HW])
        ST = p.sb([HC, 4, 18, 6])
        GN = p.sb([HC, 4, 2])
        s_x = p.sems(8)
        with p.block() as blk:
            @blk.sync
            def _(e):
                for i in range(4):
                    for h in range(2):
                        e.dma_start(X[:, i, h * 4608:(h + 1) * 4608],
                                    k.x_v[i // 2, i % 2, :, h * 4608:(h + 1) * 4608]).then_inc(s_x[2 * i + h], 16)

            @blk.vector
            def _(e):
                for i in range(4):
                    for h in range(2):
                        take(e, s_x[2 * i + h], 16)
                        for j in range(9 * h, 9 * h + 9):
                            e.bn_stats(ST[:, i, j, :], X[:, i, j * 512:(j + 1) * 512])
        group_norm_terms(nc, k, ST, 18, GN)

        WR = p.sb([HC, 2, CM])
        WO = p.sb([HM, 2, 4, HM])
        BR = p.sb([HM, 2])
        BO = p.sb([HM, 4])
        KX = p.sb([HM, 1])
        PXR = p.sb([HM, NP])
        XN = p.sb([HC, 2, 2, NP])
        XR = p.sb([HM, 2, 2, NP])
        SY = p.sb([HM, 2, 2, NP])
        SX = p.sb([HM, 2, 2, NP])
        XT = p.sb([W, 2, RC * CM])
        OY = p.sb([W, 2, RC * CM])
        Z = p.sb([W, 4, CM])
        MM = p.sb([W, 2, 2 * NCH])
        MX = p.sb([W, 2])
        FL = p.sb([1, 8])
        PB = p.ps([HM, 2, 512])
        PC = p.ps([HM, 4, 512])
        PT = p.ps([W, 2, 512])
        PTv = PT[:, :, 0:2 * CM]
        (s_w, s_v, s_xn, s_b, s_xr, s_tx, s_cy, s_cx, s_sy, s_ty, s_pt, s_o1, s_o2, s_z, s_zs,
         s_m, s_mt) = p.sems(17)
        s_wr = p.sems(3)
        s_st1 = p.sems(2)
        s_sx = p.sems(2)
        s_st2 = p.sems(2)
        chunks = [(c // NCH, c % NCH) for c in range(B * NCH)]
        N = len(chunks)
        with p.block() as blk:
            @blk.sync
            def _(e):
                for dst, src in ((WR[:, :, :], k.d["w_reduceT"].rearrange("(k p) o -> p k o", p=HC)),
                                 (WO[:, :, :, :], k.d["w_offT"].rearrange("(k p) t o -> p k t o", p=HM)),
                                 (BR[:, :], k.d["b_reduceT"]),
                                 (BO[:, :], k.d["b_offT"]), (KX[:, :], k.d["c_kx"]), (PXR[:, :], k.d["c_pxr"])):
                    e.dma_start(dst, src).then_inc(s_w, 16)
                take(e, s_w, 96)
                for s in s_wr:
                    e.sem_inc(s, 1)
                take(e, s_z)
                for b in range(B):
                    for r0 in (0, PADT + H):
                        e.dma_start(k.d["xrT"][b, r0:r0 + 4].rearrange("r p c -> p r c"), Z[:, :, :]).then_inc(s_zs, 16)
                for c, (b, r) in enumerate(chunks):
                    y0 = RC * r
                    q = c % 2
                    take(e, s_o1)
                    e.dma_start(k.d["xrT"][b, PADT + y0:PADT + y0 + RC].rearrange("r p c -> p r c"),
                                XT[:, q, :].rearrange("p (r c) -> p r c", r=RC)).then_inc(s_st1[q], 16)
                    for conv in range(2):
                        e.dma_start(k.d["sxd"][b, y0:y0 + RC, conv].rearrange("y k x -> k y x"),
                                    SX[:, q, conv, :].rearrange("k (y x) -> k y x", y=RC)).then_inc(s_sx[q], 16)
                    take(e, s_o2)
                    e.dma_start(k.d["oyd"][b, y0:y0 + RC].rearrange("r p c -> p r c"),
                                OY[:, q, :].rearrange("p (r c) -> p r c", r=RC)).then_inc(s_st2[q], 16)
                take(e, s_zs, 64)

            @blk.scalar
            def _(e):
                def norm(c):
                    b, r = chunks[c]
                    for ch in range(2):
                        e.activation(XN[:, c % 2, ch, :], X[:, 2 * b + ch, r * NP:(r + 1) * NP], ACT.Identity,
                                     bias=GN[:, 2 * b + ch, 1:2], scale=GN[:, 2 * b + ch, 0:1]).then_inc(s_xn, 1)

                take(e, s_wr[0])
                norm(0)
                for c in range(N):
                    if c + 1 < N:
                        norm(c + 1)
                    take(e, s_b)
                    for h in range(2):
                        e.activation(XR[:, c % 2, h, :], PB[:, h, 0:NP], ACT.Identity,
                                     bias=BR[:, h:h + 1]).then_inc(s_xr, 1)
                    take(e, s_cy)
                    for h in range(2):
                        e.activation(SY[:, c % 2, h, :], PC[:, 2 + h, 0:NP], ACT.Identity,
                                     bias=BO[:, 2 + h:3 + h]).then_inc(s_sy, 1)

            @blk.tensor
            def _(e):
                def reduce(c):
                    take(e, s_xn, 2)
                    for h in range(2):
                        for kc in range(2):
                            ins = e.matmul(PB[:, h, 0:NP], WR[:, kc, h * HM:(h + 1) * HM], XN[:, c % 2, kc, :],
                                           start=(kc == 0), stop=(kc == 1))
                    ins.then_inc(s_b, 1)

                def offsets(c, tiles, sem):
                    for t in tiles:
                        for kc in range(2):
                            ins = e.matmul(PC[:, t, 0:NP], WO[:, kc, t, :], XR[:, c % 2, kc, :],
                                           start=(kc == 0), stop=(kc == 1))
                    ins.then_inc(sem, 1)

                def turn(src, sem):
                    take(e, s_pt)
                    for r in range(RC):
                        for h in range(2):
                            o = (r % 2) * CM + h * HM
                            ins = e.transpose(PT[:, r // 2, o:o + HM], src[:, h, r * W:(r + 1) * W],
                                              k.ident[0:HM, 0:HM])
                    ins.then_inc(sem, 1)

                take(e, s_wr[1])
                reduce(0)
                for c in range(N):
                    take(e, s_xr, 2)
                    offsets(c, (2, 3), s_cy)
                    turn(XR[:, c % 2], s_tx)
                    offsets(c, (0, 1), s_cx)
                    if c + 1 < N:
                        reduce(c + 1)
                    take(e, s_sy, 2)
                    turn(SY[:, c % 2], s_ty)
                take(e, s_m)
                for i in range(2):
                    ins = e.transpose(PT[0:1, i, 0:W], MX[:, i:i + 1], k.ident[0:W, 0:W])
                ins.then_inc(s_mt, 1)

            @blk.vector
            def _(e):
                e.memset(Z[:, :, :], 0.0).then_inc(s_z, 1)
                for q in range(2):
                    e.sem_inc(s_st1[q], 16)
                    e.sem_inc(s_sx[q], 32)
                    e.sem_inc(s_st2[q], 16)
                e.sem_inc(s_pt, 1)
                take(e, s_wr[2])
                for i in range(2):
                    e.tensor_tensor(BO[:, i:i + 1], BO[:, i:i + 1], KX[:, :], ALU.add).then_inc(s_v, 1)
                take(e, s_v, 2)
                for c in range(N):
                    q = c % 2
                    take(e, s_st1[q], 16)
                    take(e, s_tx)
                    e.tensor_copy(XT[:, q, :].rearrange("p (u v) -> p u v", u=2), PTv).then_inc(s_pt, 1)
                    take(e, s_sx[q], 32)
                    take(e, s_cx)
                    for h in range(2):
                        ins = e.scalar_tensor_tensor(out=SX[:, q, h, :], in0=PC[:, h, 0:NP], scalar=BO[:, h:h + 1],
                                                     in1=PXR[:, :], op0=ALU.add, op1=ALU.add)
                    ins.then_inc(s_o1, 1)
                    take(e, s_st2[q], 16)
                    take(e, s_ty)
                    e.tensor_reduce(MM[:, 0, c:c + 1], PTv, AX.XY, ALU.max)
                    e.tensor_reduce(MM[:, 1, c:c + 1], PTv, AX.XY, ALU.min)
                    e.tensor_copy(OY[:, q, :].rearrange("p (u v) -> p u v", u=2), PTv).then_inc(s_o2, 1)
                    p.tick(e, s_pt)
                take(e, s_pt)
                e.tensor_reduce(MX[:, 0:1], MM[:, 0, :], AX.X, ALU.max)
                e.tensor_reduce(MX[:, 1:2], MM[:, 1, :], AX.X, ALU.min).then_inc(s_m, 1)
                take(e, s_mt)
                e.tensor_reduce(FL[:, 0:1], PT[0:1, 0, 0:W], AX.X, ALU.max).then_inc(s_v, 1)
                e.tensor_reduce(FL[:, 1:2], PT[0:1, 1, 0:W], AX.X, ALU.min).then_inc(s_v, 1)
                take(e, s_v, 2)
                e.tensor_scalar(FL[:, 2:3], FL[:, 0:1], FAR, None, ALU.is_gt).then_inc(s_v, 1)
                e.tensor_scalar(FL[:, 3:4], FL[:, 1:2], -FAR, None, ALU.is_lt).then_inc(s_v, 1)
                take(e, s_v, 2)
                e.tensor_tensor(FL[:, 2:3], FL[:, 2:3], FL[:, 3:4], ALU.max).then_inc(s_v, 1)
                take(e, s_v)
                for i, (m, a) in enumerate(((NWIN - 1.0, 1.0), (-1.0, 1.0), (2.0, 0.0), (float(H * NWIN), 0.0))):
                    e.tensor_scalar(FL[:, 4 + i:5 + i], FL[:, 2:3], m, a, ALU.mult, ALU.add).then_inc(s_v, 1)
                take(e, s_v, 4)
                e.tensor_copy(k.FLAG[:, :], FL[:, 4:8]).then_inc(s_v, 1)
                take(e, s_v)
                for q in range(2):
                    take(e, s_st1[q], 16)
                    take(e, s_sx[q], 32)
                    take(e, s_st2[q], 16)


def sample_and_convolve(nc, k):
    NB = 2 * NG
    NRB = 2
    NBB = NB * NRB
    NPX = TAPS * W
    with Phase(nc, "dc") as p:
        WD = p.sb([81, 2, 2, NG, CM])
        XW = p.sb([W, 2, 9, CM])
        OYT = p.sb([W, 2, CM])
        TAB = p.sb([W, 2, 8])
        BX = p.sb([W, 5, 2, NPX])
        HX = p.sb([W, 4, NPX])
        HY = p.sb([W, 2, CM, WIN])
        Zt = p.sb([W, 2, TAPS * WIN * CG])
        VA = p.sb([W, 2, TAPS * CG])
        VT = p.sb([81, 2, 2 * W])
        ACC = p.sb([HM, 2, 4, W])
        QX = p.sb([W, 1])
        PT = [p.ps([W, 3, 512]) for _ in range(2)]
        PR = p.ps([81, 512])
        PF = p.ps([HM, 512])
        s_w, s_hy, s_ab, s_hx, s_t, s_z, s_va, s_tr, s_vt, s_bxf, s_f, s_ff, s_out, s_fin = p.sems(14)
        s_xw = p.sems(2)
        s_row = p.sems(2)
        s_bx = p.sems(5)
        s_wr = p.sems(2)
        s_st = p.sems(2)

        def loops(e, body):
            nw = e.value_load(k.FLAG[0:1, 0:1], min_val=1, max_val=NWIN)
            for b in range(B):
                with e.Fori(0, H // NRB) as y2:
                    with e.Fori(0, nw) as w:
                        body(b, y2, w)

        with p.block() as blk:
            @blk.sync
            def _(e):
                e.dma_start(WD[:, :, :, :, :], k.d["w_dcn"]).then_inc(s_w, 16)
                e.dma_start(QX[:, :], k.d["c_qx"]).then_inc(s_w, 16)
                take(e, s_w, 32)
                for s in s_wr:
                    e.sem_inc(s, 1)
                e.sem_inc(s_bxf, 4)
                near = e.value_load(k.FLAG[0:1, 1:2], min_val=0, max_val=1)
                s0 = e.value_load(k.FLAG[0:1, 2:3], min_val=0, max_val=2)
                t0 = e.value_load(k.FLAG[0:1, 3:4], min_val=0, max_val=H * NWIN)

                def row_loads(i, b, first, ti, y):
                    e.dma_start(XW[:, i, :, :], k.d["xrT"][b, DS(first, 9)].rearrange("r p c -> p r c"))\
                        .then_inc(s_xw[i], 16)
                    e.dma_start(OYT[:, i, :], k.d["oyd"][b, DS(y, 1)].rearrange("a p c -> (a p) c")).then_inc(s_row[i], 16)
                    e.dma_start(TAB[:, i, :],
                                k.d["c_tab"][DS(ti, 1)].rearrange("a p c -> (a p) c")).then_inc(s_row[i], 16)

                def pair_load(j2, b, y, q):
                    src = k.d["sxd"][b, DS(y, 1)].rearrange("a c (q k) x -> (a c q) (k x)", q=5)
                    src = src[q:q + 1, :].partition_broadcast(W)
                    e.dma_start(BX[:, j2 % 5, :, :].rearrange("p u n -> p (u n)"), src)\
                        .then_inc(s_bx[j2 % 5], 16)

                def store_row(i, at, sem):
                    take(e, s_out, 2)
                    dst = k.d["fd"][DS(at, 1)].rearrange("y c (h p) x -> p (c h) (y x)", p=HM)
                    e.dma_start(dst, ACC[:, i, :, :]).then_inc(sem, 16)

                def body(b, y2, w):
                    for i in range(NRB):
                        y = e.snap(y2 * NRB + i)
                        first = e.snap(y * near + w * WIN + s0)
                        ti = e.snap(y * NWIN + w + t0)
                        for q in range(10):
                            take(e, s_bxf)
                            if q == 0:
                                row_loads(i, b, first, ti, y)
                            pair_load(q, b, y, q)
                            if q == 6:
                                done = y if i == 1 else e.snap(y2 * NRB + ((w + 15) >> 4) * 2)
                                store_row(1 - i, e.snap(done + b * H), s_st[1 - i])

                loops(e, body)
                take(e, s_bxf)
                row_loads(0, 0, 0, 0, 0)
                pair_load(0, 0, 0, 0)
                take(e, s_bxf)
                pair_load(1, 0, 0, 1)
                store_row(1, B * H, s_fin)
                take(e, s_fin, 16)
                take(e, s_bxf, 2)

            @blk.scalar
            def _(e):
                take(e, s_wr[0])

                def hats(i, j):
                    if j == 0:
                        take(e, s_row[i], 32)
                        for r in range(WIN):
                            e.activation(HY[:, i, :, r], OYT[:, i, :], ACT.Abs, bias=TAB[:, i, r:r + 1])\
                                .then_inc(s_ab, 1)
                        take(e, s_ab, WIN)
                        e.activation(HY[:, i, :, :], HY[:, i, :, :], ACT.Relu, bias=1.0, scale=-1.0)\
                            .then_inc(s_hy, 1)
                    q, u = (j // 2) % 5, j % 2
                    if u == 0:
                        take(e, s_bx[q], 16)
                    e.activation(BX[:, q, u, :], BX[:, q, u, :], ACT.Abs, bias=QX[:, 0:1]).then_inc(s_ab, 1)
                    take(e, s_ab)
                    e.activation(HX[:, j % 4, :], BX[:, q, u, :], ACT.Relu, bias=1.0, scale=-1.0)\
                        .then_inc(s_hx, 1)

                for j in range(3):
                    hats(0, j)

                def body(b, y2, w):
                    for n in range(NBB):
                        take(e, s_tr)
                        e.activation(VT[:, n % 2, :], PR[:, 0:2 * W], ACT.Copy).then_inc(s_vt, 1)
                        m = (n + 3) % NBB
                        hats(m // NB, m % NB)

                loops(e, body)

            @blk.tensor
            def _(e):
                take(e, s_wr[1])

                def sample(i, j):
                    g = j % NG
                    if j == 0:
                        take(e, s_xw[i], 16)
                    take(e, s_hx)
                    for t in range(TAPS):
                        ky = t // 3
                        ins = e.matmul(PT[j % 2][:, t // 3, (t % 3) * 126:(t % 3 + 1) * 126],
                                       HX[:, j % 4, t * W:(t + 1) * W],
                                       XW[:, i, ky:ky + WIN, g * CG:(g + 1) * CG],
                                       start=True, stop=True)
                    ins.then_inc(s_t, 1)

                sample(0, 0)
                sample(0, 1)

                def body(b, y2, w):
                    for n in range(NBB):
                        j, m = n % NB, (n + 2) % NBB
                        conv, g = j // NG, j % NG
                        take(e, s_va)
                        for h in range(2):
                            ins = e.transpose(PR[:, h * W:(h + 1) * W], VA[:, n % 2, h * 81:(h + 1) * 81],
                                              k.ident[0:W, 0:W])
                        ins.then_inc(s_tr, 1)
                        sample(m // NB, m % NB)
                        take(e, s_vt)
                        if g == 0:
                            take(e, s_ff)
                        for oh in range(2):
                            for h in range(2):
                                ins = e.matmul(PF[:, (2 * conv + oh) * W:(2 * conv + oh + 1) * W],
                                               WD[:, h, conv, g, oh * HM:(oh + 1) * HM],
                                               VT[:, n % 2, h * W:(h + 1) * W],
                                               start=(g == 0 and oh == 0 and h == 0), stop=(g == NG - 1 and h == 1),
                                               skip_group_check=True)
                        if g == NG - 1:
                            ins.then_inc(s_f, 1)
                        elif j % 2 == 0:
                            ins.then_inc(s_bxf, 1)

                loops(e, body)
                take(e, s_ff)
                take(e, s_hx)

            @blk.vector
            def _(e):
                e.sem_inc(s_st[0], 16)
                e.sem_inc(s_ff, 1)
                e.memset(ACC[:, :, :, :], 0.0).then_inc(s_out, 2)

                def add_up(i, conv):
                    take(e, s_f)
                    if conv == 0:
                        take(e, s_st[i], 16)
                    a = ACC[:, i, 2 * conv:2 * conv + 2, :].rearrange("p a x -> p (a x)")
                    e.scalar_tensor_tensor(out=a, in0=a, scalar=TAB[0:HM, i, 7:8],
                                           in1=PF[:, 2 * conv * W:(2 * conv + 2) * W],
                                           op0=ALU.mult, op1=ALU.add).then_inc(s_out, 1)
                    p.tick(e, s_ff)

                def body(b, y2, w):
                    for n in range(NBB):
                        i, j = n // NB, n % NB
                        if j == 0:
                            take(e, s_hy)
                        take(e, s_t)
                        hy = HY[:, i, :, :].rearrange("p c r -> p (c r)")[:, j * 63:(j + 1) * 63]
                        e.tensor_tensor(
                            Zt[:, n % 2, :].rearrange("p (b m i) -> p b m i", b=3, i=CG),
                            PT[n % 2][:, :, 0:378].rearrange("p b (m i) -> p b m i", i=CG),
                            hy.rearrange("p (b m) -> p b m", b=3).unsqueeze(3).to_broadcast([W, 3, 21, CG]),
                            ALU.mult).then_inc(s_z, 1)
                        take(e, s_z)
                        e.tensor_reduce(VA[:, n % 2, :].rearrange("p (t i) -> p t i", t=TAPS),
                                        Zt[:, n % 2, :].rearrange("p (t r i) -> p t i r", t=TAPS, r=WIN),
                                        AX.X, ALU.add).then_inc(s_va, 1)
                        if n == 10:
                            add_up(0, 0)
                        elif n == 20:
                            add_up(0, 1)
                        elif n == 30:
                            add_up(1, 0)
                    add_up(1, 1)

                loops(e, body)
                take(e, s_t, 2)
                take(e, s_hy)
                take(e, s_st[0], 16)


def mix_and_expand(nc, k):
    RC = 4
    NP = RC * W
    NCH = H // RC
    QR = H // 4
    with Phase(nc, "mx") as p:
        FB = p.sb([HM, H, 4, W])
        XI = p.sb([HC, 2, 2, NP])
        XO = p.sb([HC, 2, 2, NP])
        G0 = p.sb([HM, 2, 2, NP])
        G1 = p.sb([HM, 2, 2, NP])
        WE = p.sb([HM, 2, C])
        BE = p.sb([HC, 2])
        BD = p.sb([HM, 4])
        WA = p.sb([HM, 2, 2])
        BA = p.sb([1, 2])
        ON = p.sb([1, HM])
        SM = p.sb([HM, 4, 4])
        MN = p.sb([HM, 4])
        FA = p.sb([HM, 2])
        L = p.sb([1, 8])
        AT = p.sb([HM, 2])
        BB = p.sb([HM, 2])
        PL = p.ps([HM, 512])
        PE = [p.ps([HC, 2, 512]) for _ in range(2)]
        (s_w, s_v, s_fa, s_l, s_at, s_ab, s_g0, s_g1, s_pe, s_xo, s_bb, s_lx, s_ex, s_fbf) = p.sems(14)
        s_wr = p.sems(3)
        s_fb = p.sems(4)
        s_xi = p.sems(2)
        s_xf = p.sems(2)
        s_st = p.sems(2)
        chunks = [(c // NCH, c % NCH) for c in range(B * NCH)]
        N = len(chunks)

        def store(e, c):
            b, r = chunks[c]
            q = c % 2
            e.dma_start(k.d["x1"][b, :, :, r * NP:(r + 1) * NP].rearrange("h p n -> p h n"), XO[:, q, :, :])\
                .then_inc(s_st[q], 16)

        with p.block() as blk:
            @blk.sync
            def _(e):
                for dst, src in ((WE[:, :, :], k.d["w_expT"].rearrange("(h p) o -> p h o", p=HM)), (BE[:, :], k.d["b_expT"]),
                                 (BD[:, :], k.d["b_dcnT"]), (WA[:, :, :], k.d["w_attnT"].rearrange("(h p) o -> p h o", p=HM)),
                                 (BA[:, :], k.d["b_attn"]), (ON[:, :], k.d["c_ones"][0:1, 0:HM])):
                    e.dma_start(dst, src).then_inc(s_w, 16)
                take(e, s_w, 96)
                for s in s_wr:
                    e.sem_inc(s, 1)
                for b in range(B):
                    if b:
                        take(e, s_fbf)
                    for i in range(4):
                        r0 = 1 + b * H + i * QR
                        e.dma_start(FB[:, i * QR:(i + 1) * QR, :, :],
                                    k.d["fd"][r0:r0 + QR].rearrange("y c (h p) x -> p (y c h) x", p=HM))\
                            .then_inc(s_fb[i], 16)
                    for r in range(NCH):
                        c = b * NCH + r
                        q = c % 2
                        take(e, s_xf[q])
                        e.dma_start(XI[:, q, :, :], k.x_v[b, :, :, r * NP:(r + 1) * NP].rearrange("h p n -> p h n"))\
                            .then_inc(s_xi[q], 16)

            @blk.scalar
            def _(e):
                take(e, s_wr[0])
                for b in range(B):
                    take(e, s_lx)
                    e.activation(L[:, 4:6], L[:, 4:6], ACT.Exp).then_inc(s_ex, 1)
                    take(e, s_bb)
                    for r in range(NCH):
                        c = b * NCH + r
                        q = c % 2
                        for h in range(2):
                            e.activation(G0[:, q, h, :].rearrange("p (y x) -> p y x", x=W),
                                         FB[:, r * RC:(r + 1) * RC, h, :], ACT.Identity,
                                         bias=BB[:, h:h + 1], scale=AT[:, 1:2]).then_inc(s_g0, 1)
                        if c >= 1:
                            take(e, s_xo)
                            store(e, c - 1)
                take(e, s_xo)
                store(e, N - 1)
                for q in range(2):
                    take(e, s_st[q], 16)

            @blk.tensor
            def _(e):
                take(e, s_wr[1])
                for b in range(B):
                    take(e, s_fa)
                    for h in range(2):
                        ins = e.matmul(PL[0:1, 0:2], FA[:, h:h + 1], WA[:, h, :], start=(h == 0), stop=(h == 1))
                    ins.then_inc(s_l, 1)
                    take(e, s_at)
                    e.matmul(PL[:, 4:6], ON[:, :], L[:, 4:6], start=True, stop=True).then_inc(s_ab, 1)
                    for r in range(NCH):
                        c = b * NCH + r
                        q = c % 2
                        take(e, s_g1)
                        for m in range(2):
                            for h in range(2):
                                ins = e.matmul(PE[q][:, m, 0:NP], WE[:, h, m * HC:(m + 1) * HC], G1[:, q, h, :],
                                               start=(h == 0), stop=(h == 1))
                        ins.then_inc(s_pe, 1)

            @blk.vector
            def _(e):
                def chained(ins):
                    ins.then_inc(s_v, 1)
                    take(e, s_v)

                take(e, s_wr[2])
                for q in range(2):
                    e.sem_inc(s_xf[q], 1)
                for b in range(B):
                    for i in range(4):
                        take(e, s_fb[i], 16)
                        e.tensor_reduce(SM[:, i, :],
                                        FB[:, i * QR:(i + 1) * QR, :, :].rearrange("p y c x -> p c y x"),
                                        AX.XY, ALU.add).then_inc(s_v, 1)
                    take(e, s_v, 4)
                    chained(e.tensor_reduce(MN[:, :], SM[:, :, :].rearrange("p i c -> p c i"), AX.X, ALU.add))
                    chained(e.scalar_tensor_tensor(out=MN[:, :], in0=MN[:, :], scalar=1.0 / HW, in1=BD[:, :],
                                                   op0=ALU.mult, op1=ALU.add))
                    e.tensor_tensor(FA[:, :], MN[:, 0:2], MN[:, 2:4], ALU.add).then_inc(s_fa, 1)
                    take(e, s_l)
                    chained(e.tensor_tensor(L[:, 0:2], PL[0:1, 0:2], BA[:, :], ALU.add))
                    chained(e.tensor_reduce(L[:, 2:3], L[:, 0:2], AX.X, ALU.max))
                    e.tensor_scalar(L[:, 4:6], L[:, 0:2], L[:, 2:3], None, ALU.subtract).then_inc(s_lx, 1)
                    take(e, s_ex)
                    chained(e.tensor_reduce(L[:, 2:3], L[:, 4:6], AX.X, ALU.add))
                    chained(e.reciprocal(L[:, 3:4], L[:, 2:3]))
                    e.tensor_scalar(L[:, 4:6], L[:, 4:6], L[:, 3:4], None, ALU.mult).then_inc(s_at, 1)
                    take(e, s_ab)
                    chained(e.tensor_copy(AT[:, :], PL[:, 4:6]))
                    chained(e.tensor_scalar(BB[:, :], BD[:, 0:2], AT[:, 1:2], None, ALU.mult))
                    e.scalar_tensor_tensor(out=BB[:, :], in0=BD[:, 2:4], scalar=AT[:, 0:1], in1=BB[:, :],
                                           op0=ALU.mult, op1=ALU.add).then_inc(s_bb, 1)

                    def expand(c):
                        q = c % 2
                        take(e, s_pe)
                        take(e, s_xi[q], 16)
                        if c >= 2:
                            take(e, s_st[q], 16)
                        for m in range(2):
                            e.scalar_tensor_tensor(out=XO[:, q, m, :], in0=PE[q][:, m, 0:NP], scalar=BE[:, m:m + 1],
                                                   in1=XI[:, q, m, :], op0=ALU.add, op1=ALU.add).then_inc(s_v, 1)
                        take(e, s_v, 2)
                        bb, r = chunks[c]
                        for m in range(2):
                            ins = e.bn_stats(k.ST[:, 2 * bb + m, r, :], XO[:, q, m, :])
                        ins.then_inc(s_xo, 1)
                        p.tick(e, s_xf[q])

                    for r in range(NCH):
                        c = b * NCH + r
                        q = c % 2
                        take(e, s_g0, 2)
                        for h in range(2):
                            ins = e.scalar_tensor_tensor(out=G1[:, q, h, :].rearrange("p (y x) -> p y x", x=W),
                                                         in0=FB[:, r * RC:(r + 1) * RC, 2 + h, :], scalar=AT[:, 0:1],
                                                         in1=G0[:, q, h, :].rearrange("p (y x) -> p y x", x=W),
                                                         op0=ALU.mult, op1=ALU.add)
                        ins.then_inc(s_g1, 1)
                        if r >= 1:
                            expand(c - 1)
                    expand(b * NCH + NCH - 1)
                    if b + 1 < B:
                        p.tick(e, s_fbf)
                for q in range(2):
                    take(e, s_xf[q])


def edges_and_merge(nc, k):
    RC = 4
    NP = RC * W
    NCH = H // RC
    WP = W + 2
    with Phase(nc, "ed") as p:
        GN = p.sb([HC, 4, 2])
        group_norm_terms(nc, k, k.ST, NCH, GN)
        X1 = p.sb([HC, 2, HW])
        XP = p.sb([HC, 2, (H + 2) * WP])
        T1 = p.sb([HC, 2, 2, NP])
        T2 = p.sb([HC, 2, 2, NP])
        E = p.sb([HC, 2, 2, NP])
        XO = p.sb([HC, 2, 2, NP])
        WM = p.sb([HC, 2, C])
        BM = p.sb([HC, 2])
        PE = [p.ps([HC, 2, 512]) for _ in range(2)]
        s_w, s_v, s_z, s_xn, s_t, s_e, s_pe, s_xo, s_bf, s_tf, s_x1f = p.sems(11)
        s_wr = p.sems(2)
        s_x1 = p.sems(4)
        s_st = p.sems(2)
        QR = H // 4
        XPv = XP[:, :, :].rearrange("p h (y x) -> p h y x", x=WP)
        chunks = [(c // NCH, c % NCH) for c in range(B * NCH)]

        def at(r, dy, dx, h):
            return XPv[:, h, r * RC + 1 + dy:r * RC + 1 + dy + RC, 1 + dx:1 + dx + W]

        def tile(T, q, h):
            return T[:, q, h, :].rearrange("p (y x) -> p y x", x=W)

        with p.block() as blk:
            @blk.sync
            def _(e):
                e.dma_start(WM[:, :, :], k.d["w_mergeT"].rearrange("(h p) o -> p h o", p=HC)).then_inc(s_w, 16)
                e.dma_start(BM[:, :], k.d["b_mergeT"]).then_inc(s_w, 16)
                take(e, s_w, 32)
                for s in s_wr:
                    e.sem_inc(s, 1)
                for b in range(B):
                    if b:
                        take(e, s_x1f)
                    for i in range(4):
                        n0, n1 = i * QR * W, (i + 1) * QR * W
                        e.dma_start(X1[:, :, n0:n1], k.d["x1"][b, :, :, n0:n1].rearrange("h p n -> p h n"))\
                            .then_inc(s_x1[i], 16)
                    for r in range(NCH):
                        c = b * NCH + r
                        q = c % 2
                        take(e, s_xo)
                        e.dma_start(k.d["x2"][b, :, :, r * NP:(r + 1) * NP].rearrange("h p n -> p h n"), XO[:, q, :, :])\
                            .then_inc(s_st[q], 16)
                for q in range(2):
                    take(e, s_st[q], 16)

            @blk.scalar
            def _(e):
                take(e, s_z)
                for b in range(B):
                    if b:
                        take(e, s_bf)
                    for i in range(4):
                        take(e, s_x1[i], 16)
                        for h in range(2):
                            e.activation(XPv[:, h, 1 + i * QR:1 + (i + 1) * QR, 1:1 + W],
                                         X1[:, h, i * QR * W:(i + 1) * QR * W].rearrange("p (y x) -> p y x", x=W),
                                         ACT.Identity, bias=GN[:, 2 * b + h, 1:2],
                                         scale=GN[:, 2 * b + h, 0:1]).then_inc(s_xn, 1)

            @blk.gpsimd
            def _(e):
                e.memset(XP[:, :, :], 0.0).then_inc(s_z, 1)
                for c, (b, r) in enumerate(chunks):
                    q = c % 2
                    if r == 0:
                        take(e, s_xn, 2)
                    elif r % (NCH // 4) == NCH // 4 - 1 and r < NCH - 1:
                        take(e, s_xn, 2)
                    if c >= 2:
                        take(e, s_tf)
                    for h in range(2):
                        e.tensor_tensor(tile(T1, q, h), at(r, -1, 0, h), at(r, 1, 0, h), ALU.add)
                        ins = e.tensor_tensor(tile(T2, q, h), at(r, 0, -1, h), at(r, 0, 1, h), ALU.add)
                    ins.then_inc(s_t, 1)

            @blk.tensor
            def _(e):
                take(e, s_wr[0])
                for c in range(len(chunks)):
                    q = c % 2
                    take(e, s_e)
                    for m in range(2):
                        for h in range(2):
                            ins = e.matmul(PE[q][:, m, 0:NP], WM[:, h, m * HC:(m + 1) * HC], E[:, q, h, :],
                                           start=(h == 0), stop=(h == 1))
                    ins.then_inc(s_pe, 1)

            @blk.vector
            def _(e):
                take(e, s_wr[1])

                def merge(c):
                    b, r = chunks[c]
                    q = c % 2
                    take(e, s_pe)
                    if c >= 2:
                        take(e, s_st[q], 16)
                    for m in range(2):
                        e.scalar_tensor_tensor(out=XO[:, q, m, :], in0=PE[q][:, m, 0:NP], scalar=BM[:, m:m + 1],
                                               in1=X1[:, m, r * NP:(r + 1) * NP],
                                               op0=ALU.add, op1=ALU.add).then_inc(s_v, 1)
                    take(e, s_v, 2)
                    for m in range(2):
                        ins = e.bn_stats(k.ST[:, 2 * b + m, r, :], XO[:, q, m, :])
                    ins.then_inc(s_xo, 1)

                for c, (b, r) in enumerate(chunks):
                    q = c % 2
                    take(e, s_t)
                    for h in range(2):
                        e.tensor_tensor(T1[:, q, h, :], T1[:, q, h, :], T2[:, q, h, :], ALU.add).then_inc(s_v, 1)
                    take(e, s_v, 2)
                    for h in range(2):
                        ins = e.scalar_tensor_tensor(out=tile(E, q, h), in0=at(r, 0, 0, h), scalar=5.0,
                                                     in1=tile(T1, q, h), op0=ALU.mult, op1=ALU.subtract)
                    ins.then_inc(s_e, 1)
                    if c + 2 < len(chunks):
                        p.tick(e, s_tf)
                    if r == NCH - 1 and b + 1 < B:
                        p.tick(e, s_bf)
                    if r >= 1:
                        merge(c - 1)
                    if r == NCH - 1:
                        merge(c)
                        if b + 1 < B:
                            p.tick(e, s_x1f)


def wkv(nc, k):
    T = 512
    NCH = HW // T
    with Phase(nc, "wk") as p:
        GN = p.sb([HC, 4, 2])
        group_norm_terms(nc, k, k.ST, 24, GN)
        XI = p.sb([HC, 4, 2, T])
        XN = p.sb([HC, 2, 2, T])
        KT = p.sb([HC, 2, 2, T])
        VT = p.sb([HC, 2, 2, T])
        A2 = p.sb([HC, 2, 2, T])
        B2 = p.sb([HC, 2, 2, T])
        DP = p.sb([HC, 2, 2, T])
        AO = p.sb([HC, 2, 2, T])
        BO = p.sb([HC, 2, 2, T])
        B2V = p.sb([HC, 2, 2, T])
        BV = p.sb([HC, 2, 2, T])
        T1 = p.sb([HC, 2, T])
        T3 = p.sb([HC, 2, T])
        Y = p.sb([HC, 2, 2, T])
        S = p.sb([HC, 4, 3, 2, T + 1])
        WK = p.sb([HC, 2, C])
        WV = p.sb([HC, 2, C])
        WD = p.sb([HC, 2])
        U = p.sb([HC, 2])
        PK = [p.ps([HC, 2, T]) for _ in range(2)]
        PV = [p.ps([HC, 2, T]) for _ in range(2)]
        (s_w, s_v, s_va, s_xn, s_kv, s_k, s_o, s_ad, s_b2, s_e, s_p, s_y, s_bf, s_wd) = p.sems(14)
        s_wr = p.sems(3)
        s_xi = p.sems(4)
        s_st = p.sems(2)
        units = [(s, c) for c in range(NCH) for s in range(4)]
        N = len(units)

        def place(n):
            s, c = units[n]
            back = s % 2
            return s // 2, back, (NCH - 1 - c if back else c) * T

        with p.block() as blk:
            @blk.sync
            def _(e):
                for dst, src in ((WK[:, :, :], k.d["w_kT"].rearrange("(h p) o -> p h o", p=HC)),
                                 (WV[:, :, :], k.d["w_vT"].rearrange("(h p) o -> p h o", p=HC)),
                                 (WD[:, :], k.d["w_decayT"]), (U[:, :], k.d["uT"])):
                    e.dma_start(dst, src).then_inc(s_w, 16)
                take(e, s_w, 64)
                for s in s_wr:
                    e.sem_inc(s, 1)

                def load(n):
                    b, _b, t0 = place(n)
                    e.dma_start(XI[:, n % 4, :, :], k.d["x2"][b, :, :, t0:t0 + T].rearrange("h p n -> p h n"))\
                        .then_inc(s_xi[n % 4], 16)

                for n in range(3):
                    load(n)
                for n in range(N):
                    take(e, s_y)
                    b, back, t0 = place(n)
                    dst = k.d["ybd"] if back else k.d["yfd"]
                    e.dma_start(dst[b, :, :, t0:t0 + T].rearrange("h p n -> p h n"), Y[:, n % 2, :, :])\
                        .then_inc(s_st[n % 2], 16)
                    if n + 3 < N:
                        load(n + 3)
                for q in range(2):
                    take(e, s_st[q], 16)

            @blk.scalar
            def _(e):
                take(e, s_wr[0])
                e.activation(WD[:, :], WD[:, :], ACT.Exp).then_inc(s_wd, 1)

                def norm(n):
                    b, back, _t = place(n)
                    take(e, s_xi[n % 4], 16)
                    for h in range(2):
                        x = XI[:, n % 4, h, ::-1] if back else XI[:, n % 4, h, :]
                        ins = e.activation(XN[:, n % 2, h, :], x, ACT.Identity,
                                           bias=GN[:, 2 * b + h, 1:2], scale=GN[:, 2 * b + h, 0:1])
                    ins.then_inc(s_xn, 1)

                norm(0)
                for n in range(N):
                    q = n % 2
                    if n + 1 < N:
                        norm(n + 1)
                    if n >= 2:
                        take(e, s_bf)
                    take(e, s_kv)
                    e.activation(VT[:, q, :, :], PV[q][:, :, :], ACT.Copy)
                    e.activation(KT[:, q, :, :], PK[q][:, :, :], ACT.Copy).then_inc(s_k, 1)
                    take(e, s_ad)
                    e.activation(AO[:, q, :, :], DP[:, q, :, :], ACT.Relu).then_inc(s_va, 1)
                    e.activation(BO[:, q, :, :], DP[:, q, :, :], ACT.Relu, scale=-1.0).then_inc(s_va, 1)
                    e.activation(A2[:, q, :, :], A2[:, q, :, :], ACT.Exp)
                    take(e, s_va, 2)
                    e.activation(AO[:, q, :, :], AO[:, q, :, :], ACT.Exp, scale=-1.0)
                    e.activation(BO[:, q, :, :], BO[:, q, :, :], ACT.Exp, scale=-1.0)
                    take(e, s_b2)
                    e.activation(B2[:, q, :, :], B2[:, q, :, :], ACT.Exp).then_inc(s_e, 1)
                take(e, s_bf, 2)

            @blk.tensor
            def _(e):
                take(e, s_wr[1])
                for n in range(N):
                    q = n % 2
                    take(e, s_xn)
                    for P_, W_ in ((PV[q], WV), (PK[q], WK)):
                        for m in range(2):
                            for h in range(2):
                                ins = e.matmul(P_[:, m, :], W_[:, h, m * HC:(m + 1) * HC], XN[:, q, h, :],
                                               start=(h == 0), stop=(h == 1))
                    ins.then_inc(s_kv, 1)

            @blk.gpsimd
            def _(e):
                def spread(n):
                    q = n % 2
                    take(e, s_o)
                    s = units[n][0]
                    e.tensor_tensor(B2[:, q, :, :], KT[:, q, :, :], S[:, s, 0, :, 1:T + 1], ALU.subtract)\
                        .then_inc(s_b2, 1)

                def weigh(n):
                    q = n % 2
                    take(e, s_e)
                    e.tensor_tensor(B2V[:, q, :, :], B2[:, q, :, :], VT[:, q, :, :], ALU.mult)
                    e.tensor_tensor(BV[:, q, :, :], BO[:, q, :, :], VT[:, q, :, :], ALU.mult).then_inc(s_p, 1)

                for n in range(N + 1):
                    if n < N:
                        spread(n)
                    if n >= 1:
                        weigh(n - 1)

            @blk.vector
            def _(e):
                take(e, s_wr[2])
                take(e, s_wd)
                e.tensor_scalar(WD[:, :], WD[:, :], -1.0, None, ALU.mult).then_inc(s_v, 1)
                e.memset(S[:, :, 0, :, T:T + 1], -1e38).then_inc(s_v, 1)
                e.memset(S[:, :, 1:3, :, T:T + 1], 0.0).then_inc(s_v, 1)
                take(e, s_v, 3)
                for q in range(2):
                    e.sem_inc(s_st[q], 16)

                def maxima(n):
                    q = n % 2
                    s = units[n][0]
                    take(e, s_k)
                    e.tensor_copy(S[:, s, :, :, 0:1], S[:, s, :, :, T:T + 1]).then_inc(s_v, 1)
                    take(e, s_v)
                    for m in range(2):
                        e.tensor_tensor_scan(S[:, s, 0, m, 1:T + 1], WD[:, m:m + 1].to_broadcast([HC, T]),
                                             KT[:, q, m, :], S[:, s, 0, m, 0:1], ALU.add, ALU.max).then_inc(s_v, 1)
                    take(e, s_v, 2)
                    for m in range(2):
                        ins = e.scalar_tensor_tensor(out=DP[:, q, m, :], in0=KT[:, q, m, :], scalar=U[:, m:m + 1],
                                                     in1=S[:, s, 0, m, 0:T], op0=ALU.add, op1=ALU.subtract)
                    ins.then_inc(s_o, 1)
                    for m in range(2):
                        ins = e.scalar_tensor_tensor(out=A2[:, q, m, :], in0=S[:, s, 0, m, 0:T],
                                                     scalar=WD[:, m:m + 1], in1=S[:, s, 0, m, 1:T + 1],
                                                     op0=ALU.add, op1=ALU.subtract)
                    ins.then_inc(s_ad, 1)

                def sums(n):
                    q = n % 2
                    s = units[n][0]
                    back = place(n)[1]
                    take(e, s_p)
                    for i, D in ((1, B2V), (2, B2)):
                        for m in range(2):
                            e.tensor_tensor_scan(S[:, s, i, m, 1:T + 1], A2[:, q, m, :], D[:, q, m, :],
                                                 S[:, s, i, m, 0:1], ALU.mult, ALU.add).then_inc(s_v, 1)
                    take(e, s_v, 4)
                    e.tensor_tensor(T1[:, :, :], AO[:, q, :, :], S[:, s, 1, :, 0:T], ALU.mult).then_inc(s_v, 1)
                    e.tensor_tensor(T3[:, :, :], AO[:, q, :, :], S[:, s, 2, :, 0:T], ALU.mult).then_inc(s_v, 1)
                    take(e, s_v, 2)
                    e.tensor_tensor(T3[:, :, :], T3[:, :, :], BO[:, q, :, :], ALU.add).then_inc(s_v, 1)
                    e.tensor_tensor(T1[:, :, :], T1[:, :, :], BV[:, q, :, :], ALU.add).then_inc(s_v, 1)
                    take(e, s_v, 2)
                    e.reciprocal(T3[:, :, :], T3[:, :, :]).then_inc(s_v, 1)
                    take(e, s_v)
                    take(e, s_st[q], 16)
                    y = Y[:, q, :, ::-1] if back else Y[:, q, :, :]
                    e.tensor_tensor(y, T1[:, :, :], T3[:, :, :], ALU.mult).then_inc(s_y, 1)
                    p.tick(e, s_bf)

                for n in range(N + 1):
                    if n < N:
                        maxima(n)
                    if n >= 1:
                        sums(n - 1)


def gate_and_project(nc, k):
    T = 512
    NCH = HW // T
    with Phase(nc, "gp") as p:
        GN = p.sb([HC, 4, 2])
        group_norm_terms(nc, k, k.ST, 24, GN)
        XI = p.sb([HC, 4, 2, T])
        YF = p.sb([HC, 4, 2, T])
        YB = p.sb([HC, 4, 2, T])
        XN = p.sb([HC, 2, 2, T])
        SG = p.sb([HC, 2, 2, T])
        HH = p.sb([HC, 3, 2, T])
        SQ = p.sb([HC, 2, 2, T])
        RS = p.sb([HC, 2, T])
        HN = p.sb([HC, 2, 2, T])
        XO = p.sb([HC, 2, 2, T])
        WR = p.sb([HC, 2, C])
        WO = p.sb([HC, 2, C])
        GB = p.sb([HC, 2, 2])
        AV = p.sb([HC, HC])
        PR = p.ps([HC, 2, T])
        PM = [p.ps([HC, T]) for _ in range(2)]
        PV = [p.ps([HC, T]) for _ in range(2)]
        PO = p.ps([HC, 2, T])
        (s_w, s_v, s_xn, s_r, s_sg, s_s, s_h, s_m, s_d, s_sq, s_var, s_ve, s_sd, s_hn, s_af, s_po, s_xo,
         s_xf) = p.sems(18)
        s_wr = p.sems(3)
        s_xi = p.sems(4)
        s_yy = p.sems(4)
        s_st = p.sems(2)
        N = B * NCH

        with p.block() as blk:
            @blk.sync
            def _(e):
                for dst, src in ((WR[:, :, :], k.d["w_rT"].rearrange("(h p) o -> p h o", p=HC)),
                                 (WO[:, :, :], k.d["w_oT"].rearrange("(h p) o -> p h o", p=HC)),
                                 (GB[:, :, :], k.d["ln_T"]), (AV[:, :], k.d["c_avg"])):
                    e.dma_start(dst, src).then_inc(s_w, 16)
                take(e, s_w, 64)
                for s in s_wr:
                    e.sem_inc(s, 1)

                def load(n):
                    b, t0 = n // NCH, n % NCH * T
                    i = n % 4
                    e.dma_start(XI[:, i, :, :], k.d["x2"][b, :, :, t0:t0 + T].rearrange("h p n -> p h n"))\
                        .then_inc(s_xi[i], 16)
                    for Y_, src in ((YF, k.d["yfd"]), (YB, k.d["ybd"])):
                        e.dma_start(Y_[:, i, :, :], src[b, :, :, t0:t0 + T].rearrange("h p n -> p h n"))\
                            .then_inc(s_yy[i], 16)

                for n in range(3):
                    load(n)
                for n in range(N):
                    b, t0 = n // NCH, n % NCH * T
                    if n >= 1 and n + 2 < N:
                        load(n + 2)
                    take(e, s_xo)
                    e.dma_start(k.d["x3"][b, :, :, t0:t0 + T].rearrange("h p n -> p h n"), XO[:, n % 2, :, :])\
                        .then_inc(s_st[n % 2], 16)
                for q in range(2):
                    take(e, s_st[q], 16)

            @blk.scalar
            def _(e):
                take(e, s_wr[0])
                for n in range(N + 2):
                    if n < N:
                        b = n // NCH
                        take(e, s_xi[n % 4], 16)
                        for h in range(2):
                            ins = e.activation(XN[:, n % 2, h, :], XI[:, n % 4, h, :], ACT.Identity,
                                               bias=GN[:, 2 * b + h, 1:2], scale=GN[:, 2 * b + h, 0:1])
                        ins.then_inc(s_xn, 1)
                        take(e, s_r)
                        e.activation(SG[:, n % 2, :, :], PR[:, :, :], ACT.Sigmoid).then_inc(s_sg, 1)
                    if 1 <= n <= N:
                        take(e, s_d)
                        e.activation(SQ[:, (n - 1) % 2, :, :], HH[:, (n - 1) % 3, :, :], ACT.Square).then_inc(s_sq, 1)
                    if n >= 2:
                        q = n % 2
                        take(e, s_ve)
                        e.activation(RS[:, q, :], RS[:, q, :], ACT.Sqrt).then_inc(s_sd, 1)
                        take(e, s_hn)
                        for h in range(2):
                            ins = e.activation(HN[:, q, h, :], HN[:, q, h, :], ACT.Identity,
                                               bias=GB[:, h, 1:2], scale=GB[:, h, 0:1])
                        ins.then_inc(s_af, 1)

            @blk.tensor
            def _(e):
                take(e, s_wr[1])

                def project(P_, W_, X_, sem):
                    for m in range(2):
                        for h in range(2):
                            ins = e.matmul(P_[:, m, :], W_[:, h, m * HC:(m + 1) * HC], X_[:, h, :],
                                           start=(h == 0), stop=(h == 1))
                    ins.then_inc(sem, 1)

                def average(P_, X_, sem):
                    for h in range(2):
                        ins = e.matmul(P_[:, :], AV[:, :], X_[:, h, :], start=(h == 0), stop=(h == 1))
                    ins.then_inc(sem, 1)

                for n in range(N + 2):
                    if n < N:
                        take(e, s_xn)
                        project(PR, WR, XN[:, n % 2], s_r)
                        take(e, s_h)
                        average(PM[n % 2], HH[:, n % 3], s_m)
                    if 1 <= n <= N:
                        take(e, s_sq)
                        average(PV[(n - 1) % 2], SQ[:, (n - 1) % 2], s_var)
                    if n >= 2:
                        take(e, s_af)
                        project(PO, WO, HN[:, n % 2], s_po)

            @blk.gpsimd
            def _(e):
                for n in range(N):
                    i = n % 4
                    take(e, s_yy[i], 32)
                    if n >= 4:
                        take(e, s_xf)
                    e.tensor_tensor(YF[:, i, :, :], YF[:, i, :, :], YB[:, i, :, :], ALU.add).then_inc(s_s, 1)

            @blk.vector
            def _(e):
                take(e, s_wr[2])
                for q in range(2):
                    e.sem_inc(s_st[q], 16)
                for n in range(N + 2):
                    if n < N:
                        take(e, s_s)
                        take(e, s_sg)
                        e.scalar_tensor_tensor(out=HH[:, n % 3, :, :], in0=YF[:, n % 4, :, :], scalar=0.5,
                                               in1=SG[:, n % 2, :, :], op0=ALU.mult, op1=ALU.mult).then_inc(s_h, 1)
                    if 1 <= n <= N:
                        i = (n - 1) % 3
                        take(e, s_m)
                        e.tensor_tensor(HH[:, i, :, :], HH[:, i, :, :],
                                        PM[(n - 1) % 2][:, :].unsqueeze(1).to_broadcast([HC, 2, T]),
                                        ALU.subtract).then_inc(s_d, 1)
                    if n >= 2:
                        q, i = n % 2, (n - 2) % 3
                        take(e, s_var)
                        e.tensor_scalar(RS[:, q, :], PV[q][:, :], EPS, None, ALU.add).then_inc(s_ve, 1)
                        take(e, s_sd)
                        e.reciprocal(RS[:, q, :], RS[:, q, :]).then_inc(s_v, 1)
                        take(e, s_v)
                        e.tensor_tensor(HN[:, q, :, :], HH[:, i, :, :],
                                        RS[:, q, :].unsqueeze(1).to_broadcast([HC, 2, T]),
                                        ALU.mult).then_inc(s_hn, 1)
                        take(e, s_po)
                        take(e, s_st[q], 16)
                        e.tensor_tensor(XO[:, q, :, :], PO[:, :, :], XI[:, (n - 2) % 4, :, :], ALU.add)\
                            .then_inc(s_v, 1)
                        take(e, s_v)
                        b, c = (n - 2) // NCH, (n - 2) % NCH
                        for m in range(2):
                            ins = e.bn_stats(k.ST2[:, 2 * b + m, c, :], XO[:, q, m, :])
                        ins.then_inc(s_xo, 1)
                        if n - 2 + 4 < N:
                            p.tick(e, s_xf)


DI = 2 * C
ND = DI // 128
RK = 12
NS = 16


def mamba_inputs(nc, k):
    T = 512
    NCH = HW // T
    with Phase(nc, "mi") as p:
        GN = p.sb([HC, 4, 2])
        group_norm_terms(nc, k, k.ST2, 18, GN)
        XI = p.sb([HC, 3, 2, T])
        XN = p.sb([HC, 2, 2, T])
        XH = p.sb([128, 2, ND, T + 3])
        CV = p.sb([128, 2, ND, T])
        XV = p.sb([128, 2, ND, T])
        SZ = p.sb([128, 2, ND, T])
        XD = p.sb([RK + 2 * NS, 2, T])
        XS = p.sb([128, 2, ND, T])
        EE = p.sb([128, 2, ND, T])
        UU = p.sb([128, 2, ND, T])
        PP = p.sb([128, 2, ND, T])
        PM = p.sb([128, ND, T])
        DL = p.sb([128, 2, ND, T])
        WI = p.sb([HC, 2, 2 * DI])
        WX = p.sb([128, ND, RK + 2 * NS])
        WT = p.sb([RK, DI])
        CW = p.sb([128, ND, 4])
        CB = p.sb([128, ND])
        BT = p.sb([128, ND])
        PX = p.ps([128, ND, T])
        PZ = p.ps([128, ND, T])
        PD = p.ps([RK + 2 * NS, T])
        (s_w, s_v, s_va, s_xn, s_px, s_pz, s_xh, s_cv, s_xv, s_pd, s_xd, s_xd2, s_dt, s_xs, s_ex, s_ln, s_zf,
         s_so, s_sx, s_dt2, s_pzf, s_p, s_pp, s_pe) = p.sems(24)
        s_wr = p.sems(3)
        s_xi = p.sems(3)
        s_sxv, s_ssz, s_sxd, s_sdl = (p.sems(2) for _ in range(4))
        N = B * NCH

        def flat(t, q):
            return t[:, q, :, :].rearrange("p d t -> p (d t)")

        def by_tile(ap, b, t0):
            return ap[b, :, t0:t0 + T].rearrange("(d p) t -> p d t", p=128)

        with p.block() as blk:
            @blk.sync
            def _(e):
                for dst, src in ((WI[:, :, :], k.d["w_inT"].rearrange("(h p) o -> p h o", p=HC)),
                                 (WX[:, :, :], k.d["w_xT"].rearrange("(d p) o -> p d o", p=128)),
                                 (WT[:, :], k.d["w_dtT"]), (CW[:, :, :], k.d["conv_wT"]), (CB[:, :], k.d["conv_bT"]),
                                 (BT[:, :], k.d["b_dtT"])):
                    e.dma_start(dst, src).then_inc(s_w, 16)
                take(e, s_w, 96)
                for s in s_wr:
                    e.sem_inc(s, 1)

                def load(n):
                    b, t0 = n // NCH, n % NCH * T
                    e.dma_start(XI[:, n % 3, :, :], k.d["x3"][b, :, :, t0:t0 + T].rearrange("h p n -> p h n"))\
                        .then_inc(s_xi[n % 3], 16)

                load(0)
                load(1)
                for n in range(N):
                    b, t0, q = n // NCH, n % NCH * T, n % 2
                    take(e, s_sx)
                    e.dma_start(by_tile(k.d["szd"], b, t0), SZ[:, q, :, :]).then_inc(s_ssz[q], 16)
                    e.dma_start(by_tile(k.d["xvd"], b, t0), XV[:, q, :, :]).then_inc(s_sxv[q], 16)
                    if n + 2 < N:
                        load(n + 2)
                    take(e, s_xd2)
                    e.dma_start(k.d["bcd"][b, :, t0:t0 + T], XD[RK:, q, :]).then_inc(s_sxd[q], 16)
                    take(e, s_so)
                    e.dma_start(by_tile(k.d["dld"], b, t0), DL[:, q, :, :]).then_inc(s_sdl[q], 16)

            @blk.scalar
            def _(e):
                take(e, s_wr[0])
                for q in range(2):
                    e.sem_inc(s_ssz[q], 16)
                    e.sem_inc(s_sxv[q], 16)
                    e.sem_inc(s_sdl[q], 16)

                def norm(n):
                    b = n // NCH
                    take(e, s_xi[n % 3], 16)
                    for h in range(2):
                        ins = e.activation(XN[:, n % 2, h, :], XI[:, n % 3, h, :], ACT.Identity,
                                           bias=GN[:, 2 * b + h, 1:2], scale=GN[:, 2 * b + h, 0:1])
                    ins.then_inc(s_xn, 1)

                def fill(n):
                    take(e, s_px)
                    e.activation(XH[:, n % 2, :, 3:T + 3], PX[:, :, :], ACT.Copy).then_inc(s_xh, 1)

                norm(0)
                fill(0)
                for n in range(N):
                    q = n % 2
                    if n + 1 < N:
                        norm(n + 1)
                    take(e, s_pz)
                    take(e, s_ssz[q], 16)
                    e.activation(SZ[:, q, :, :], PZ[:, :, :], ACT.Silu).then_inc(s_zf, 1)
                    take(e, s_cv)
                    take(e, s_sxv[q], 16)
                    e.activation(XV[:, q, :, :], CV[:, q, :, :], ACT.Silu).then_inc(s_xv, 1)
                    if n + 1 < N:
                        fill(n + 1)
                    take(e, s_xs)
                    e.activation(EE[:, q, :, :], XS[:, q, :, :], ACT.Abs).then_inc(s_va, 1)
                    take(e, s_va)
                    e.activation(EE[:, q, :, :], EE[:, q, :, :], ACT.Exp, scale=-1.0).then_inc(s_ex, 1)
                    take(e, s_ln)
                    take(e, s_sdl[q], 16)
                    e.activation(DL[:, q, :, :], UU[:, q, :, :], ACT.Ln).then_inc(s_va, 1)
                    take(e, s_va)
                    e.sem_inc(s_dt2, 1)
                for q in range(2):
                    take(e, s_ssz[q], 16)
                    take(e, s_sxv[q], 16)
                    take(e, s_sdl[q], 16)

            @blk.tensor
            def _(e):
                take(e, s_wr[1])

                def inner(n, P_, first, sem):
                    for d in range(ND):
                        for h in range(2):
                            o = first + d * 128
                            ins = e.matmul(P_[:, d, :], WI[:, h, o:o + 128], XN[:, n % 2, h, :],
                                           start=(h == 0), stop=(h == 1))
                    ins.then_inc(sem, 1)

                take(e, s_xn)
                inner(0, PX, 0, s_px)
                for n in range(N):
                    q = n % 2
                    inner(n, PZ, DI, s_pz)
                    take(e, s_zf)
                    take(e, s_xv)
                    for d in range(ND):
                        ins = e.matmul(PD[:, :], WX[:, d, :], XV[:, q, d, :], start=(d == 0), stop=(d == ND - 1))
                    ins.then_inc(s_pd, 1)
                    if n + 1 < N:
                        take(e, s_xn)
                        inner(n + 1, PX, 0, s_px)
                    take(e, s_xd)
                    for d in range(ND):
                        ins = e.matmul(PZ[:, d, :], WT[:, d * 128:(d + 1) * 128], XD[0:RK, q, :],
                                       start=True, stop=True)
                    ins.then_inc(s_dt, 1)
                    take(e, s_pzf)

            @blk.gpsimd
            def _(e):
                for n in range(N):
                    q = n % 2
                    take(e, s_pe)
                    e.tensor_scalar(PP[:, q, :, :], EE[:, q, :, :], 1.0 / 3.0, -0.5, ALU.mult, ALU.add)\
                        .then_inc(s_p, 1)
                    e.tensor_scalar(PM[:, :, :], EE[:, q, :, :], NEAR1, None, ALU.is_le).then_inc(s_p, 1)
                    take(e, s_p, 2)
                    e.tensor_tensor(PP[:, q, :, :], PP[:, q, :, :], EE[:, q, :, :], ALU.mult).then_inc(s_p, 1)
                    e.tensor_tensor(PM[:, :, :], PM[:, :, :], EE[:, q, :, :], ALU.mult).then_inc(s_p, 1)
                    take(e, s_p, 2)
                    e.tensor_scalar(PP[:, q, :, :], PP[:, q, :, :], 1.0, None, ALU.add).then_inc(s_p, 1)
                    e.tensor_scalar(XS[:, q, :, :], XS[:, q, :, :], 0.0, None, ALU.max).then_inc(s_p, 1)
                    take(e, s_p, 2)
                    e.tensor_tensor(PP[:, q, :, :], PP[:, q, :, :], PM[:, :, :], ALU.mult).then_inc(s_p, 1)
                    take(e, s_p)
                    e.tensor_tensor(PP[:, q, :, :], PP[:, q, :, :], XS[:, q, :, :], ALU.add).then_inc(s_pp, 1)

            @blk.vector
            def _(e):
                take(e, s_wr[2])
                e.memset(XH[:, 1, :, T:T + 3], 0.0).then_inc(s_v, 1)
                take(e, s_v)
                for q in range(2):
                    e.sem_inc(s_sxd[q], 16)

                def conv(n):
                    q = n % 2
                    if n % NCH == 0 and n:
                        e.memset(XH[:, q, :, 0:3], 0.0).then_inc(s_v, 1)
                    else:
                        e.tensor_copy(XH[:, q, :, 0:3], XH[:, 1 - q, :, T:T + 3]).then_inc(s_v, 1)
                    take(e, s_xh)
                    take(e, s_v)
                    for d in range(ND):
                        e.tensor_scalar(CV[:, q, d, :], XH[:, q, d, 3:3 + T], CW[:, d, 3:4], CB[:, d:d + 1],
                                        ALU.mult, ALU.add).then_inc(s_v, 1)
                    for j in range(3):
                        take(e, s_v, 3)
                        for d in range(ND):
                            ins = e.scalar_tensor_tensor(out=CV[:, q, d, :], in0=XH[:, q, d, j:j + T],
                                                         scalar=CW[:, d, j:j + 1], in1=CV[:, q, d, :],
                                                         op0=ALU.mult, op1=ALU.add)
                            if j < 2:
                                ins.then_inc(s_v, 1)
                    ins.then_inc(s_cv, 1)

                conv(0)
                for n in range(N):
                    q = n % 2
                    take(e, s_sxd[q], 16)
                    take(e, s_pd)
                    e.tensor_copy(XD[:, q, :], PD[:, :]).then_inc(s_xd, 1)
                    p.tick(e, s_xd2)
                    p.tick(e, s_sx)
                    take(e, s_dt)
                    for d in range(ND):
                        ins = e.tensor_scalar(XS[:, q, d, :], PZ[:, d, :], BT[:, d:d + 1], BT[:, d:d + 1],
                                              ALU.add, ALU.add)
                    ins.then_inc(s_xs, 1)
                    p.tick(e, s_pzf)
                    if n + 1 < N:
                        conv(n + 1)
                    take(e, s_ex)
                    e.tensor_scalar(UU[:, q, :, :], EE[:, q, :, :], 1.0, None, ALU.add).then_inc(s_ln, 1)
                    p.tick(e, s_pe)
                    take(e, s_dt2)
                    take(e, s_pp)
                    e.scalar_tensor_tensor(out=flat(UU, q), in0=flat(EE, q), scalar=NEAR1, in1=flat(DL, q),
                                           op0=ALU.is_gt, op1=ALU.mult).then_inc(s_v, 1)
                    take(e, s_v)
                    e.tensor_tensor(DL[:, q, :, :], UU[:, q, :, :], PP[:, q, :, :], ALU.add).then_inc(s_so, 1)
                for q in range(2):
                    take(e, s_sxd[q], 16)


def mamba_scan(nc, k):
    T = 512
    NCH = HW // T
    NC = B * NCH
    N = NC * NS
    RB, RA, RG = 6, 3, 3
    with Phase(nc, "ms") as p:
        XV = p.sb([128, 2, ND, T])
        DL = p.sb([128, 2, ND, T])
        SZ = p.sb([128, 2, ND, T])
        DU = p.sb([128, 2, ND, T])
        XI = p.sb([HC, 2, 2, T])
        BC = p.sb([128, RB, 2, T])
        DB = p.sb([128, RB, ND, T])
        DA = p.sb([128, RA, ND, T])
        HH = p.sb([128, 3, ND, T])
        G = p.sb([128, RG, ND, T])
        YY = p.sb([128, ND, T])
        XO = p.sb([HC, 2, 2, T])
        TKP = p.sb([128, 1])
        CAR = p.sb([128, NS, ND])
        AL = p.sb([128, ND, NS])
        DD = p.sb([128, ND])
        WO = p.sb([128, ND, C])
        PY = [p.ps([128, ND, T]) for _ in range(2)]
        PO = p.ps([HC, 2, T])
        (s_w, s_v, s_c, s_al, s_da, s_bu, s_g, s_ra, s_rb, s_rg, s_yz, s_po, s_xo, s_y1, s_du, s_dp) = p.sems(16)
        s_wr = p.sems(3)
        s_bc = p.sems(RB)
        s_in = p.sems(2)
        s_st = p.sems(2)

        with p.block() as blk:
            @blk.sync
            def _(e):
                for dst, src in ((AL[:, :, :], k.d["a_log"].rearrange("(d p) n -> p d n", p=128)), (DD[:, :], k.d["d_T"]),
                                 (WO[:, :, :], k.d["w_outT"].rearrange("(d p) o -> p d o", p=128))):
                    e.dma_start(dst, src).then_inc(s_w, 16)
                take(e, s_w, 48)
                for s in s_wr:
                    e.sem_inc(s, 1)

                def load(c):
                    b, t0, q = c // NCH, c % NCH * T, c % 2
                    for dst, src in ((DL, k.d["dld"]), (XV, k.d["xvd"]), (SZ, k.d["szd"])):
                        e.dma_start(dst[:, q, :, :], src[b, :, t0:t0 + T].rearrange("(d p) t -> p d t", p=128))\
                            .then_inc(s_in[q], 16)
                    e.dma_start(XI[:, q, :, :], k.d["x3"][b, :, :, t0:t0 + T].rearrange("h p n -> p h n"))\
                        .then_inc(s_in[q], 16)

                def spread(i):
                    c, n = i // NS, i % NS
                    b, t0 = c // NCH, c % NCH * T
                    if i >= RB:
                        take(e, s_rb)
                    src = k.d["bcd"][b, n:n + NS + 1:NS, t0:t0 + T]
                    e.dma_start(BC[:, i % RB, :, :], src.unsqueeze(0).to_broadcast([128, 2, T]))\
                        .then_inc(s_bc[i % RB], 16)

                load(0)
                load(1)
                for i in range(N + 2 * NS):
                    if i < N:
                        spread(i)
                    c, n = i // NS - 1, i % NS
                    if n == 13 and 0 <= c < NC:
                        b, t0 = c // NCH, c % NCH * T
                        take(e, s_xo)
                        e.dma_start(k.out_v[b, :, :, t0:t0 + T].rearrange("h p n -> p h n"), XO[:, c % 2, :, :])\
                            .then_inc(s_st[c % 2], 16)
                        if c + 2 < NC:
                            load(c + 2)
                for q in range(2):
                    take(e, s_st[q], 16)
                take(e, s_rb, RB)

            @blk.scalar
            def _(e):
                take(e, s_wr[0])
                e.activation(AL[:, :, :], AL[:, :, :], ACT.Exp).then_inc(s_al, 1)
                take(e, s_y1)
                for i in range(N):
                    c, n = i // NS, i % NS
                    if n == 0:
                        take(e, s_du)
                    if i >= RA:
                        take(e, s_ra)
                    for d in range(ND):
                        ins = e.activation(DA[:, i % RA, d, :], DL[:, c % 2, d, :], ACT.Exp, scale=AL[:, d, n:n + 1])
                    ins.then_inc(s_da, 1)
                take(e, s_ra, RA)

            @blk.gpsimd
            def _(e):
                def gain(c):
                    q = c % 2
                    take(e, s_in[q], 64)
                    e.tensor_tensor(DU[:, q, :, :], DL[:, q, :, :], XV[:, q, :, :], ALU.mult).then_inc(s_du, 1)
                    e.tensor_tensor(TKP[:, :], TKP[:, :], TKP[:, :], ALU.mult).then_inc(s_dp, 1)
                    take(e, s_dp)

                e.memset(TKP[:, :], 0.0).then_inc(s_dp, 1)
                take(e, s_dp)
                gain(0)
                for i in range(N):
                    c, n = i // NS, i % NS
                    if n == 15 and c + 1 < NC:
                        gain(c + 1)
                    take(e, s_bc[i % RB], 16)
                    e.tensor_tensor(DB[:, i % RB, :, :], DU[:, c % 2, :, :],
                                    BC[:, i % RB, 0, :].unsqueeze(1).to_broadcast([128, ND, T]),
                                    ALU.mult).then_inc(s_bu, 1)

            @blk.tensor
            def _(e):
                take(e, s_wr[1])
                for i in range(N + NS):
                    c, n = i // NS, i % NS
                    if i < N:
                        take(e, s_g)
                        for d, sem in enumerate((s_ra, s_rb, s_rg)):
                            e.matmul(PY[c % 2][:, d, :], k.ident[:, :], G[:, i % RG, d, :], start=(n == 0),
                                     stop=(n == NS - 1)).then_inc(sem, 1)
                    if n == 5 and c >= 1:
                        take(e, s_yz)
                        for m in range(2):
                            for d in range(ND):
                                ins = e.matmul(PO[:, m, :], WO[:, d, m * HC:(m + 1) * HC], YY[:, d, :],
                                               start=(d == 0), stop=(d == ND - 1))
                        ins.then_inc(s_po, 1)

            @blk.vector
            def _(e):
                take(e, s_wr[2])
                take(e, s_al)
                e.tensor_scalar(AL[:, :, :], AL[:, :, :], -1.0, None, ALU.mult).then_inc(s_y1, 1)
                for q in range(2):
                    e.sem_inc(s_st[q], 16)
                e.sem_inc(s_rg, RG)
                e.memset(CAR[:, :, :], 0.0).then_inc(s_c, 1)

                def scan(i):
                    c, n = i // NS, i % NS
                    take(e, s_c)
                    take(e, s_bu)
                    take(e, s_da)
                    for d in range(ND):
                        e.tensor_tensor_scan(HH[:, i % 3, d, :], DA[:, i % RA, d, :], DB[:, i % RB, d, :],
                                             CAR[:, n, d:d + 1], ALU.mult, ALU.add).then_inc(s_v, 1)
                    take(e, s_v, ND)
                    if c % NCH == NCH - 1:
                        e.memset(CAR[:, n, :], 0.0).then_inc(s_c, 1)
                    else:
                        e.tensor_copy(CAR[:, n, :], HH[:, i % 3, :, T - 1]).then_inc(s_c, 1)

                def read(i):
                    take(e, s_rg)
                    e.tensor_tensor(G[:, i % RG, :, :], HH[:, i % 3, :, :],
                                    BC[:, i % RB, 1, :].unsqueeze(1).to_broadcast([128, ND, T]),
                                    ALU.mult).then_inc(s_g, 1)

                def finish(c):
                    q = c % 2
                    for d in range(ND):
                        e.scalar_tensor_tensor(out=YY[:, d, :], in0=XV[:, q, d, :], scalar=DD[:, d:d + 1],
                                               in1=PY[q][:, d, :], op0=ALU.mult, op1=ALU.add).then_inc(s_v, 1)
                    take(e, s_v, ND)
                    e.tensor_tensor(YY[:, :, :], YY[:, :, :], SZ[:, q, :, :], ALU.mult).then_inc(s_yz, 1)

                def put(c):
                    q = c % 2
                    take(e, s_po)
                    take(e, s_st[q], 16)
                    e.tensor_tensor(XO[:, q, :, :], PO[:, :, :], XI[:, q, :, :], ALU.add).then_inc(s_xo, 1)

                for i in range(N + NS):
                    c, n = i // NS, i % NS
                    if i < N:
                        scan(i)
                    if 1 <= i <= N:
                        read(i - 1)
                    if n == 3 and c >= 1:
                        if c == NC:
                            take(e, s_rg, RG)
                        finish(c - 1)
                    if n == 9 and c >= 1:
                        put(c - 1)
                take(e, s_c)


PHASES = (first_norm_and_projections, sample_and_convolve, mix_and_expand, edges_and_merge,
          wkv, gate_and_project, mamba_inputs, mamba_scan)


def program(nc, ins, out, phases=PHASES, kind="Internal"):
    k = Shared(ins)
    k.x_v = k.d["x"].rearrange("b (h p) y x -> b h p (y x)", p=HC)
    k.out_v = out.rearrange("b (h p) y x -> b h p (y x)", p=HC)
    scratch = {"xrT": [B, ROWS, W, CM], "sxd": [B, H, 2, HM, W], "oyd": [B, H, W, CM],
               "fd": [B * H + 3, 2, CM, W], "x1": [B, 2, HC, HW], "x2": [B, 2, HC, HW], "x3": [B, 2, HC, HW],
               "yfd": [B, 2, HC, HW], "ybd": [B, 2, HC, HW],
               "xvd": [B, DI, HW], "dld": [B, DI, HW], "szd": [B, DI, HW], "bcd": [B, 2 * NS, HW]}
    for n, shape in scratch.items():
        if n not in ins:
            k.d[n] = nc.dram_tensor(n, shape, F32, kind=kind).ap()
    with Phase(nc, "top") as p:
        k.ident = p.sb([128, 128])
        k.G6 = p.sb([HC, HC])
        k.FLAG = p.sb([1, 4], I32)
        k.ST = p.sb([HC, 4, 24, 6])
        k.ST2 = p.sb([HC, 4, 18, 6])
        k.const_loads = [(k.ident[:, :], k.d["c_ident"]), (k.G6[:, :], k.d["c_g6"])]
        load_constants(nc, k)
        for phase in phases:
            phase(nc, k)


def layout(inp):
    f = np.float32
    d = {"x": inp["x"]}
    d["w_reduceT"] = inp["L0_conv_w_reduce"].T
    d["b_reduceT"] = inp["L0_conv_b_reduce"].reshape(2, HM).T
    wo = inp["L0_conv_w_offset"].reshape(2, HM, 2, CM).transpose(3, 2, 0, 1)[:, ::-1]
    d["w_offT"] = wo.reshape(CM, 4, HM)
    d["b_offT"] = inp["L0_conv_b_offset"].reshape(2, HM, 2).transpose(1, 2, 0)[:, ::-1].reshape(HM, 4)
    wd = np.stack([inp["L0_conv_w_dcnw"], inp["L0_conv_w_dcnh"]]).reshape(2, CM, NG, CG, TAPS)
    wd = wd.transpose(4, 3, 0, 2, 1).reshape(2, 81, 2, NG, CM).transpose(1, 0, 2, 3, 4)
    d["w_dcn"] = wd
    d["w_expT"] = inp["L0_conv_w_expand"].T
    d["b_expT"] = inp["L0_conv_b_expand"].reshape(2, HC).T
    d["b_dcnT"] = np.stack([inp["L0_conv_b_dcnw"], inp["L0_conv_b_dcnh"]]).reshape(4, HM).T
    d["w_attnT"] = inp["L0_conv_w_attn"].T
    d["b_attn"] = inp["L0_conv_b_attn"][None, :]
    d["w_mergeT"] = inp["L1_conv_merge_w"].reshape(C, C).T
    d["b_mergeT"] = inp["L1_conv_merge_b"].reshape(2, HC).T
    for n in "kvro":
        d[f"w_{n}T"] = inp["L2_conv_W" + n].T
    d["w_decayT"] = inp["L2_conv_w_decay"].reshape(2, HC).T
    d["uT"] = inp["L2_conv_u"].reshape(2, HC).T
    d["ln_T"] = np.stack([inp["L2_conv_ln_g"], inp["L2_conv_ln_b"]]).reshape(2, 2, HC).transpose(2, 1, 0)
    d["c_avg"] = np.full((HC, HC), 1.0 / C, f)
    d["w_inT"] = inp["L3_conv_W_in"].T
    d["conv_wT"] = inp["L3_conv_conv_w"].reshape(ND, 128, 4).transpose(1, 0, 2)
    d["conv_bT"] = inp["L3_conv_conv_b"].reshape(ND, 128).T
    d["w_xT"] = inp["L3_conv_W_x"].T
    d["w_dtT"] = inp["L3_conv_W_dt"].T
    d["b_dtT"] = inp["L3_conv_b_dt"].reshape(ND, 128).T
    d["a_log"] = inp["L3_conv_A_log"]
    d["d_T"] = inp["L3_conv_D"].reshape(ND, 128).T
    d["w_outT"] = inp["L3_conv_W_out"].T
    d["c_ones"] = np.ones((1, 128), f)
    d["c_ident"] = np.eye(128, dtype=f)
    i = np.arange(HC) // 6
    d["c_g6"] = (i[:, None] == i[None, :]).astype(f) / f(6)
    d["c_kx"] = ((np.arange(HM) % TAPS % 3) - 1).astype(f)[:, None]
    d["c_pxr"] = np.tile(np.arange(W, dtype=f), (HM, 4))
    d["c_qx"] = -np.arange(W, dtype=f)[:, None]
    tab = np.zeros((2, H, NWIN, 8), f)
    y, w = np.arange(H)[:, None, None], np.arange(NWIN)[None, :, None]
    r = np.arange(WIN)[None, None, :]
    tab[0, :, :, :WIN] = 3 - r
    tab[1, :, :, :WIN] = y - WIN * w + 1 - r
    tab[1, :, 1:, 7] = 1
    d["c_tab"] = np.repeat(tab.reshape(-1, 1, 8), W, axis=1)
    return {n: np.ascontiguousarray(np.asarray(a)) for n, a in d.items()}


def kernel(**inputs):
    import concourse.bacc as bacc
    from concourse.bass_utils import run_bass_kernel_spmd

    nc = bacc.Bacc("TRN2", target_bir_lowering=False, num_devices=1)
    arrays = layout({n: np.asarray(a) for n, a in inputs.items()})
    ins = {n: nc.dram_tensor(n, a.shape, mybir.dt.from_np(a.dtype), kind="ExternalInput").ap()
           for n, a in arrays.items()}
    out = nc.dram_tensor("out", [B, C, H, W], F32, kind="ExternalOutput").ap()
    program(nc, ins, out)
    r = run_bass_kernel_spmd(nc, [arrays], core_ids=[0])
    return r.results[0]["out"]
```

```python
import numpy as np
import concourse.bass as bass
from concourse import mybir
from concourse.alu_op_type import AluOpType as ALU
from contextlib import ExitStack

F32 = mybir.dt.float32
I32 = mybir.dt.int32
ACT = mybir.ActivationFunctionType
AX = mybir.AxisListType
DS = bass.DynSlice

B, C, CM, H, W = 2, 192, 180, 96, 96
HW = H * W
NG, TAPS, CG = 10, 9, 18
NT = HW // 128
WIN = 8
NWIN = 13
NCK = -(-NG * TAPS * CG // 128)
FAR = 3.0
PADT = 4
ROWS = 208
EPS = 1e-5
NEAR1 = 2.0 ** -7
HC = C // 2
HM = CM // 2


def take(eng, sem, n=1):
    eng.wait_ge(sem, n).then_inc(sem, -n)


class Phase:

    def __init__(self, nc, name):
        self.nc, self.name, self.ctx, self.n = nc, name, ExitStack(), 0
        self.cell, self.turn = None, 0

    def __enter__(self):
        self.ctx.__enter__()
        return self

    def __exit__(self, *a):
        return self.ctx.__exit__(*a)

    def _name(self, kind):
        self.n += 1
        return f"{self.name}_{kind}{self.n}"

    def sb(self, shape, dt=F32):
        return self.ctx.enter_context(self.nc.sbuf_tensor(self._name("t"), shape, dt))

    def ps(self, shape):
        return self.ctx.enter_context(self.nc.psum_tensor(self._name("p"), shape, F32))

    def sem(self):
        return self.ctx.enter_context(self.nc.semaphore(self._name("s")))

    def sems(self, n):
        return [self.sem() for _ in range(n)]

    def tick(self, eng, sem):
        if self.cell is None:
            self.cell = self.sb([1, 16])
        self.turn = (self.turn + 1) % 16
        eng.memset(self.cell[:, self.turn:self.turn + 1], 0.0).then_inc(sem, 1)

    def block(self):
        return self.nc.Block()


class Shared:

    def __init__(self, tensors):
        self.d, self.n = dict(tensors), 0

    def fresh(self, name):
        self.n += 1
        return f"{name}{self.n}"


def group_norm_terms(nc, k, ST, nseg, GN):
    with Phase(nc, k.fresh("gn")) as p:
        MV = p.sb([HC, 4, 2])
        MG = p.sb([HC, 4])
        D = p.sb([HC, 4])
        Q = p.sb([HC, 4])
        V = p.sb([HC, 4])
        PM = p.ps([HC, 512])
        PV = p.ps([HC, 512])
        s_v, s_mv, s_m, s_q, s_var, s_e, s_sd = p.sems(7)
        with p.block() as blk:
            @blk.vector
            def _(e):
                for i in range(4):
                    ins = e.bn_aggr(MV[:, i, :], ST[:, i, 0:nseg, :])
                ins.then_inc(s_mv, 1)
                take(e, s_m)
                e.tensor_copy(MG[:, :], PM[:, 0:4]).then_inc(s_v, 1)
                take(e, s_v)
                e.tensor_tensor(D[:, :], MV[:, :, 0], MG[:, :], ALU.subtract).then_inc(s_v, 1)
                take(e, s_v)
                e.tensor_tensor(D[:, :], D[:, :], D[:, :], ALU.mult).then_inc(s_v, 1)
                take(e, s_v)
                e.tensor_tensor(Q[:, :], D[:, :], MV[:, :, 1], ALU.add).then_inc(s_q, 1)
                take(e, s_var)
                e.tensor_scalar(V[:, :], PV[:, 0:4], EPS, None, ALU.add).then_inc(s_e, 1)
                take(e, s_sd)
                e.reciprocal(GN[:, :, 0], V[:, :]).then_inc(s_v, 1)
                take(e, s_v)
                e.scalar_tensor_tensor(out=GN[:, :, 1], in0=MG[:, :], scalar=-1.0, in1=GN[:, :, 0],
                                       op0=ALU.mult, op1=ALU.mult)

            @blk.tensor
            def _(e):
                take(e, s_mv)
                e.matmul(PM[:, 0:4], k.G6[:, :], MV[:, :, 0], start=True, stop=True).then_inc(s_m, 1)
                take(e, s_q)
                e.matmul(PV[:, 0:4], k.G6[:, :], Q[:, :], start=True, stop=True).then_inc(s_var, 1)

            @blk.scalar
            def _(e):
                take(e, s_e)
                e.activation(V[:, :], V[:, :], ACT.Sqrt).then_inc(s_sd, 1)


def load_constants(nc, k):
    with Phase(nc, "cst") as p:
        s = p.sem()
        with p.block() as blk:
            @blk.sync
            def _(e):
                n = 0
                for dst, src in k.const_loads:
                    e.dma_start(dst, src).then_inc(s, 16)
                    n += 16
                e.wait_ge(s, n).then_inc(s, -n)


def first_norm_and_projections(nc, k):
    RC = 4
    NP = RC * W
    NCH = H // RC
    with Phase(nc, "in") as p:
        X = p.sb([HC, 4, HW])
        ST = p.sb([HC, 4, 18, 6])
        GN = p.sb([HC, 4, 2])
        s_x = p.sems(8)
        with p.block() as blk:
            @blk.sync
            def _(e):
                for i in range(4):
                    for h in range(2):
                        e.dma_start(X[:, i, h * 4608:(h + 1) * 4608],
                                    k.x_v[i // 2, i % 2, :, h * 4608:(h + 1) * 4608]).then_inc(s_x[2 * i + h], 16)

            @blk.vector
            def _(e):
                for i in range(4):
                    for h in range(2):
                        take(e, s_x[2 * i + h], 16)
                        for j in range(9 * h, 9 * h + 9):
                            e.bn_stats(ST[:, i, j, :], X[:, i, j * 512:(j + 1) * 512])
        group_norm_terms(nc, k, ST, 18, GN)

        WR = p.sb([HC, 2, CM])
        WO = p.sb([HM, 2, 4, HM])
        BR = p.sb([HM, 2])
        BO = p.sb([HM, 4])
        KX = p.sb([HM, 1])
        PXR = p.sb([HM, NP])
        XN = p.sb([HC, 2, 2, NP])
        XR = p.sb([HM, 2, 2, NP])
        SY = p.sb([HM, 2, 2, NP])
        SX = p.sb([HM, 2, 2, NP])
        XT = p.sb([W, 2, RC * CM])
        OY = p.sb([W, 2, RC * CM])
        Z = p.sb([W, 4, CM])
        MM = p.sb([W, 2, 2 * NCH])
        MX = p.sb([W, 2])
        FL = p.sb([1, 8])
        PB = p.ps([HM, 2, 512])
        PC = p.ps([HM, 4, 512])
        PT = p.ps([W, 2, 512])
        PTv = PT[:, :, 0:2 * CM]
        (s_w, s_v, s_xn, s_b, s_xr, s_tx, s_cy, s_cx, s_sy, s_ty, s_pt, s_o1, s_o2, s_z, s_zs,
         s_m, s_mt) = p.sems(17)
        s_wr = p.sems(3)
        s_st1 = p.sems(2)
        s_sx = p.sems(2)
        s_st2 = p.sems(2)
        chunks = [(c // NCH, c % NCH) for c in range(B * NCH)]
        N = len(chunks)
        with p.block() as blk:
            @blk.sync
            def _(e):
                for dst, src in ((WR[:, :, :], k.d["w_reduceT"].rearrange("(k p) o -> p k o", p=HC)),
                                 (WO[:, :, :, :], k.d["w_offT"].rearrange("(k p) t o -> p k t o", p=HM)),
                                 (BR[:, :], k.d["b_reduceT"]),
                                 (BO[:, :], k.d["b_offT"]), (KX[:, :], k.d["c_kx"]), (PXR[:, :], k.d["c_pxr"])):
                    e.dma_start(dst, src).then_inc(s_w, 16)
                take(e, s_w, 96)
                for s in s_wr:
                    e.sem_inc(s, 1)
                take(e, s_z)
                for b in range(B):
                    for r0 in (0, PADT + H, PADT + H + 4):
                        e.dma_start(k.d["xrT"][b, r0:r0 + 4].rearrange("r p c -> p r c"), Z[:, :, :]).then_inc(s_zs, 16)
                for c, (b, r) in enumerate(chunks):
                    y0 = RC * r
                    q = c % 2
                    take(e, s_o1)
                    e.dma_start(k.d["xrT"][b, PADT + y0:PADT + y0 + RC].rearrange("r p c -> p r c"),
                                XT[:, q, :].rearrange("p (r c) -> p r c", r=RC)).then_inc(s_st1[q], 16)
                    for conv in range(2):
                        e.dma_start(k.d["sxd"][b, 3 * r:3 * r + 3, conv].rearrange("i k x -> k i x"),
                                    SX[:, q, conv, :].rearrange("k (i x) -> k i x", i=3)).then_inc(s_sx[q], 16)
                    take(e, s_o2)
                    e.dma_start(k.d["oyd"][b, y0:y0 + RC].rearrange("r p c -> p r c"),
                                OY[:, q, :].rearrange("p (r c) -> p r c", r=RC)).then_inc(s_st2[q], 16)
                take(e, s_zs, 96)

            @blk.scalar
            def _(e):
                def norm(c):
                    b, r = chunks[c]
                    for ch in range(2):
                        e.activation(XN[:, c % 2, ch, :], X[:, 2 * b + ch, r * NP:(r + 1) * NP], ACT.Identity,
                                     bias=GN[:, 2 * b + ch, 1:2], scale=GN[:, 2 * b + ch, 0:1]).then_inc(s_xn, 1)

                take(e, s_wr[0])
                norm(0)
                for c in range(N):
                    if c + 1 < N:
                        norm(c + 1)
                    take(e, s_b)
                    for h in range(2):
                        e.activation(XR[:, c % 2, h, :], PB[:, h, 0:NP], ACT.Identity,
                                     bias=BR[:, h:h + 1]).then_inc(s_xr, 1)
                    take(e, s_cy)
                    for h in range(2):
                        e.activation(SY[:, c % 2, h, :], PC[:, 2 + h, 0:NP], ACT.Identity,
                                     bias=BO[:, 2 + h:3 + h]).then_inc(s_sy, 1)

            @blk.tensor
            def _(e):
                def reduce(c):
                    take(e, s_xn, 2)
                    for h in range(2):
                        for kc in range(2):
                            ins = e.matmul(PB[:, h, 0:NP], WR[:, kc, h * HM:(h + 1) * HM], XN[:, c % 2, kc, :],
                                           start=(kc == 0), stop=(kc == 1))
                    ins.then_inc(s_b, 1)

                def offsets(c, tiles, sem):
                    for t in tiles:
                        for kc in range(2):
                            ins = e.matmul(PC[:, t, 0:NP], WO[:, kc, t, :], XR[:, c % 2, kc, :],
                                           start=(kc == 0), stop=(kc == 1))
                    ins.then_inc(sem, 1)

                def turn(src, sem):
                    take(e, s_pt)
                    for r in range(RC):
                        for h in range(2):
                            o = (r % 2) * CM + h * HM
                            ins = e.transpose(PT[:, r // 2, o:o + HM], src[:, h, r * W:(r + 1) * W],
                                              k.ident[0:HM, 0:HM])
                    ins.then_inc(sem, 1)

                take(e, s_wr[1])
                reduce(0)
                for c in range(N):
                    take(e, s_xr, 2)
                    offsets(c, (2, 3), s_cy)
                    turn(XR[:, c % 2], s_tx)
                    offsets(c, (0, 1), s_cx)
                    if c + 1 < N:
                        reduce(c + 1)
                    take(e, s_sy, 2)
                    turn(SY[:, c % 2], s_ty)
                take(e, s_m)
                for i in range(2):
                    ins = e.transpose(PT[0:1, i, 0:W], MX[:, i:i + 1], k.ident[0:W, 0:W])
                ins.then_inc(s_mt, 1)

            @blk.vector
            def _(e):
                e.memset(Z[:, :, :], 0.0).then_inc(s_z, 1)
                for q in range(2):
                    e.sem_inc(s_st1[q], 16)
                    e.sem_inc(s_sx[q], 32)
                    e.sem_inc(s_st2[q], 16)
                e.sem_inc(s_pt, 1)
                take(e, s_wr[2])
                for i in range(2):
                    e.tensor_tensor(BO[:, i:i + 1], BO[:, i:i + 1], KX[:, :], ALU.add).then_inc(s_v, 1)
                take(e, s_v, 2)
                for c in range(N):
                    q = c % 2
                    take(e, s_st1[q], 16)
                    take(e, s_tx)
                    e.tensor_copy(XT[:, q, :].rearrange("p (u v) -> p u v", u=2), PTv).then_inc(s_pt, 1)
                    take(e, s_sx[q], 32)
                    take(e, s_cx)
                    for h in range(2):
                        ins = e.scalar_tensor_tensor(out=SX[:, q, h, :], in0=PC[:, h, 0:NP], scalar=BO[:, h:h + 1],
                                                     in1=PXR[:, :], op0=ALU.add, op1=ALU.add)
                    ins.then_inc(s_o1, 1)
                    take(e, s_st2[q], 16)
                    take(e, s_ty)
                    e.tensor_reduce(MM[:, 0, c:c + 1], PTv, AX.XY, ALU.max)
                    e.tensor_reduce(MM[:, 1, c:c + 1], PTv, AX.XY, ALU.min)
                    e.tensor_copy(OY[:, q, :].rearrange("p (u v) -> p u v", u=2), PTv).then_inc(s_o2, 1)
                    p.tick(e, s_pt)
                take(e, s_pt)
                e.tensor_reduce(MX[:, 0:1], MM[:, 0, :], AX.X, ALU.max)
                e.tensor_reduce(MX[:, 1:2], MM[:, 1, :], AX.X, ALU.min).then_inc(s_m, 1)
                take(e, s_mt)
                e.tensor_reduce(FL[:, 0:1], PT[0:1, 0, 0:W], AX.X, ALU.max).then_inc(s_v, 1)
                e.tensor_reduce(FL[:, 1:2], PT[0:1, 1, 0:W], AX.X, ALU.min).then_inc(s_v, 1)
                take(e, s_v, 2)
                e.tensor_scalar(FL[:, 2:3], FL[:, 0:1], FAR, None, ALU.is_gt).then_inc(s_v, 1)
                e.tensor_scalar(FL[:, 3:4], FL[:, 1:2], -FAR, None, ALU.is_lt).then_inc(s_v, 1)
                take(e, s_v, 2)
                e.tensor_tensor(FL[:, 2:3], FL[:, 2:3], FL[:, 3:4], ALU.max).then_inc(s_v, 1)
                take(e, s_v)
                for i, (m, a) in enumerate(((NWIN - 1.0, 1.0), (-1.0, 1.0), (2.0, 0.0), (float(NT * NWIN), 0.0))):
                    e.tensor_scalar(FL[:, 4 + i:5 + i], FL[:, 2:3], m, a, ALU.mult, ALU.add).then_inc(s_v, 1)
                take(e, s_v, 4)
                e.tensor_copy(k.FLAG[:, :], FL[:, 4:8]).then_inc(s_v, 1)
                take(e, s_v)
                for q in range(2):
                    take(e, s_st1[q], 16)
                    take(e, s_sx[q], 32)
                    take(e, s_st2[q], 16)


def sample_and_convolve(nc, k):
    NB = 2 * NG
    NRB = 2
    NBB = NB * NRB
    NPX = TAPS * 128
    LEN = TAPS * CG
    pieces = [range(LEN * g // 128, LEN * (g + 1) // 128) for g in range(NG - 1)]
    pieces.append(range(LEN * (NG - 1) // 128, NCK))
    with Phase(nc, "dc") as p:
        WD = p.sb([128, NCK, 2, CM])
        XW = p.sb([W, 2, WIN + 2, CM])
        OYT = p.sb([128, 2, CM])
        TAB = p.sb([128, 2, WIN + 1])
        BX = p.sb([W, 5, 2, NPX])
        HX = p.sb([W, 4, NPX])
        HY = p.sb([128, 2, CM, WIN])
        V = p.sb([128, 2, CM, WIN])
        Zt = p.sb([128, 4, WIN * LEN])
        VA = p.sb([128, 2, NG * LEN])
        VT = p.sb([128, 2, 2, 128])
        ACC = p.sb([HM, 2, 4, 128])
        QX = p.sb([W, 1])
        PT = [p.ps([128, 3, 512]) for _ in range(2)]
        PR = p.ps([128, 512])
        PF = p.ps([HM, 512])
        s_w, s_hy, s_ab, s_hx, s_t, s_z, s_va, s_tr, s_vt, s_bxf, s_f, s_ff, s_out, s_fin, s_rw, s_hyf, s_pt, s_va2 = p.sems(18)
        s_xw = p.sems(2)
        s_row = p.sems(2)
        s_bx = p.sems(5)
        s_wr = p.sems(2)
        s_st = p.sems(2)

        def loops(e, body):
            nw = e.value_load(k.FLAG[0:1, 0:1], min_val=1, max_val=NWIN)
            for b in range(B):
                with e.Fori(0, NT // NRB) as y2:
                    with e.Fori(0, nw) as w:
                        body(b, y2, w)

        with p.block() as blk:
            @blk.sync
            def _(e):
                e.dma_start(WD[:, :, :, :], k.d["w_dcn"]).then_inc(s_w, 16)
                e.dma_start(QX[:, :], k.d["c_qx"]).then_inc(s_w, 16)
                take(e, s_w, 32)
                for s in s_wr:
                    e.sem_inc(s, 1)
                e.sem_inc(s_bxf, 4)
                near = e.value_load(k.FLAG[0:1, 1:2], min_val=0, max_val=1)
                s0 = e.value_load(k.FLAG[0:1, 2:3], min_val=0, max_val=2)
                t0 = e.value_load(k.FLAG[0:1, 3:4], min_val=0, max_val=NT * NWIN)

                def tile_loads(i, b, first, ti, y):
                    e.dma_start(XW[:, i, :, :], k.d["xrT"][b, DS(first, WIN + 2)].rearrange("r p c -> p r c"))\
                        .then_inc(s_xw[i], 16)
                    e.dma_start(OYT[:, i, :], k.oyd_v[b, DS(y, 1)].rearrange("a p c -> (a p) c")).then_inc(s_row[i], 16)
                    e.dma_start(TAB[:, i, :],
                                k.d["c_tab"][DS(ti, 1)].rearrange("a p c -> (a p) c")).then_inc(s_row[i], 16)

                def pair_load(j2, b, y, q):
                    src = k.d["sxd"][b, DS(y, 1)].rearrange("a c (q k) x -> (a c q) (k x)", q=5)
                    src = src[q:q + 1, :].partition_broadcast(W)
                    e.dma_start(BX[:, j2 % 5, :, :].rearrange("p u n -> p (u n)"), src)\
                        .then_inc(s_bx[j2 % 5], 16)

                def store_tile(i, at, sem):
                    take(e, s_out, 2)
                    dst = k.d["fd"][DS(at, 1)].rearrange("y c (h p) x -> p (c h) (y x)", p=HM)
                    e.dma_start(dst, ACC[:, i, :, :]).then_inc(sem, 16)

                def body(b, y2, w):
                    for i in range(NRB):
                        y = e.snap(y2 * NRB + i)
                        first = e.snap((y + ((y * 43) >> 7)) * near + w * WIN + s0)
                        ti = e.snap(y * NWIN + w + t0)
                        for q in range(10):
                            take(e, s_bxf)
                            if q == 0:
                                tile_loads(i, b, first, ti, y)
                            pair_load(q, b, y, q)
                            if q == 6:
                                done = y if i == 1 else e.snap(y2 * NRB + ((w + 15) >> 4) * 2)
                                store_tile(1 - i, e.snap(done + b * NT), s_st[1 - i])

                loops(e, body)
                take(e, s_bxf)
                tile_loads(0, 0, 0, 0, 0)
                pair_load(0, 0, 0, 0)
                take(e, s_bxf)
                pair_load(1, 0, 0, 1)
                store_tile(1, B * NT, s_fin)
                take(e, s_fin, 16)
                take(e, s_bxf, 2)

            @blk.scalar
            def _(e):
                take(e, s_wr[0])

                def hats(j):
                    q, u = (j // 2) % 5, j % 2
                    if u == 0:
                        take(e, s_bx[q], 16)
                    e.activation(BX[:, q, u, :], BX[:, q, u, :], ACT.Abs, bias=QX[:, 0:1]).then_inc(s_ab, 1)
                    take(e, s_ab)
                    e.activation(HX[:, j % 4, :], BX[:, q, u, :], ACT.Relu, bias=1.0, scale=-1.0)\
                        .then_inc(s_hx, 1)

                def row_weights(i, step):
                    o = slice(step // 2 * HM, step // 2 * HM + HM)
                    if step == 0:
                        take(e, s_rw)
                        take(e, s_hyf)
                    if step % 2 == 0:
                        e.activation(V[:, i, o, :], V[:, i, o, :], ACT.Abs).then_inc(s_va2, 1)
                    else:
                        take(e, s_va2)
                        e.activation(HY[:, i, o, :], V[:, i, o, :], ACT.Relu, bias=1.0, scale=-1.0).then_inc(s_hy, 1)

                for step in range(4):
                    row_weights(0, step)
                for j in range(4):
                    hats(j)

                def body(b, y2, w):
                    for n in range(NBB):
                        take(e, s_tr)
                        for u, c in enumerate(pieces[n % NG]):
                            o = min(128, NG * LEN - 128 * c)
                            ins = e.activation(VT[0:o, n % 2, u, :], PR[0:o, u * 128:(u + 1) * 128], ACT.Copy)
                        ins.then_inc(s_vt, 1)
                        m = (n + 4) % NBB
                        hats(m % NB)
                        if 15 <= n % NB < 19:
                            row_weights(n // NB ^ 1, n % NB - 15)

                loops(e, body)
                take(e, s_hyf)

            @blk.tensor
            def _(e):
                take(e, s_wr[1])

                def sample(i, j):
                    g = j % NG
                    if j == 0:
                        take(e, s_xw[i], 16)
                    take(e, s_hx)
                    for t in range(TAPS):
                        ky = t // 3
                        ins = e.matmul(PT[j % 2][:, t // 3, (t % 3) * 144:(t % 3 + 1) * 144],
                                       HX[:, j % 4, t * 128:(t + 1) * 128],
                                       XW[:, i, ky:ky + WIN, g * CG:(g + 1) * CG],
                                       start=True, stop=True)
                    ins.then_inc(s_t, 1)

                sample(0, 0)
                sample(0, 1)
                take(e, s_pt)
                sample(0, 2)

                def body(b, y2, w):
                    for n in range(NBB):
                        j, m = n % NB, (n + 3) % NBB
                        conv, g = j // NG, j % NG
                        take(e, s_va)
                        for u, c in enumerate(pieces[g]):
                            o = min(128, NG * LEN - 128 * c)
                            ins = e.transpose(PR[0:o, u * 128:(u + 1) * 128],
                                              VA[:, n // NG % 2, 128 * c:128 * c + o], k.ident[:, :])
                        ins.then_inc(s_tr, 1)
                        sample(m // NB, m % NB)
                        take(e, s_vt)
                        if g == 0:
                            take(e, s_ff)
                        for u, c in enumerate(pieces[g]):
                            o = min(128, NG * LEN - 128 * c)
                            for oh in range(2):
                                ins = e.matmul(PF[:, (2 * conv + oh) * 128:(2 * conv + oh + 1) * 128],
                                               WD[0:o, c, conv, oh * HM:(oh + 1) * HM], VT[0:o, n % 2, u, :],
                                               start=(c == 0 and oh == 0), stop=(c == NCK - 1),
                                               skip_group_check=True)
                        if g == NG - 1:
                            ins.then_inc(s_f, 1)
                        elif j % 2 == 0:
                            ins.then_inc(s_bxf, 1)

                loops(e, body)
                take(e, s_ff)
                take(e, s_hx)
                take(e, s_va, 2)

            @blk.gpsimd
            def _(e):
                def rows(i):
                    take(e, s_row[i], 32)
                    e.tensor_tensor(V[:, i, :, :], OYT[:, i, :].unsqueeze(2).to_broadcast([128, CM, WIN]),
                                    TAB[:, i, 0:WIN].unsqueeze(1).to_broadcast([128, CM, WIN]), ALU.add)\
                        .then_inc(s_rw, 1)

                def body(b, y2, w):
                    for i in range(NRB):
                        rows(i)

                loops(e, body)
                rows(0)

            @blk.vector
            def _(e):
                e.sem_inc(s_st[0], 16)
                e.sem_inc(s_hyf, 2)
                e.sem_inc(s_ff, 1)
                e.memset(ACC[:, :, :, :], 0.0).then_inc(s_out, 2)

                def add_up(i, conv):
                    take(e, s_f)
                    if conv == 0:
                        take(e, s_st[i], 16)
                    a = ACC[:, i, 2 * conv:2 * conv + 2, :].rearrange("p a x -> p (a x)")
                    e.scalar_tensor_tensor(out=a, in0=a, scalar=TAB[0:HM, i, WIN:WIN + 1],
                                           in1=PF[:, 256 * conv:256 * conv + 256],
                                           op0=ALU.mult, op1=ALU.add).then_inc(s_out, 1)
                    p.tick(e, s_ff)

                def weigh(n):
                    i, j = n // NB % NRB, n % NB
                    if j % NG == 0:
                        take(e, s_hy)
                    take(e, s_t)
                    hy = HY[:, i, :, :].rearrange("p c r -> p (c r)")[:, j * 72:(j + 1) * 72]
                    e.tensor_tensor(
                        Zt[:, n % 4, :].rearrange("p (b m i) -> p b m i", b=3, i=CG),
                        PT[n % 2][:, :, 0:432].rearrange("p b (m i) -> p b m i", i=CG),
                        hy.rearrange("p (b m) -> p b m", b=3).unsqueeze(3).to_broadcast([128, 3, 24, CG]),
                        ALU.mult).then_inc(s_z, 1)
                    if j == NB - 1:
                        p.tick(e, s_hyf)

                def sum_rows(n):
                    g = n % NG
                    take(e, s_z)
                    e.tensor_reduce(VA[:, n // NG % 2, g * LEN:(g + 1) * LEN].rearrange("p (t i) -> p t i", t=TAPS),
                                    Zt[:, n % 4, :].rearrange("p (t r i) -> p t i r", t=TAPS, r=WIN),
                                    AX.X, ALU.add).then_inc(s_va, 1)

                def body(b, y2, w):
                    for n in range(2, NBB + 2):
                        weigh(n + 1)
                        if n % NG == 1:
                            add_up((n - 11) // NB, n // NG % 2 ^ 1)
                        sum_rows(n)

                weigh(0)
                p.tick(e, s_pt)
                for n in range(2):
                    weigh(n + 1)
                    sum_rows(n)
                loops(e, body)
                take(e, s_z)
                take(e, s_hy)
                take(e, s_st[0], 16)


def mix_and_expand(nc, k):
    RC = 4
    NP = RC * W
    NCH = H // RC
    QR = NT // 4
    with Phase(nc, "mx") as p:
        FB = p.sb([HM, NT, 4, 128])
        XI = p.sb([HC, 2, 2, NP])
        XO = p.sb([HC, 2, 2, NP])
        G0 = p.sb([HM, 2, 2, NP])
        G1 = p.sb([HM, 2, 2, NP])
        WE = p.sb([HM, 2, C])
        BE = p.sb([HC, 2])
        BD = p.sb([HM, 4])
        WA = p.sb([HM, 2, 2])
        BA = p.sb([1, 2])
        ON = p.sb([1, HM])
        SM = p.sb([HM, 4, 4])
        MN = p.sb([HM, 4])
        FA = p.sb([HM, 2])
        L = p.sb([1, 8])
        AT = p.sb([HM, 2])
        BB = p.sb([HM, 2])
        PL = p.ps([HM, 512])
        PE = [p.ps([HC, 2, 512]) for _ in range(2)]
        (s_w, s_v, s_fa, s_l, s_at, s_ab, s_g0, s_g1, s_pe, s_xo, s_bb, s_lx, s_ex, s_fbf) = p.sems(14)
        s_wr = p.sems(3)
        s_fb = p.sems(4)
        s_xi = p.sems(2)
        s_xf = p.sems(2)
        s_st = p.sems(2)
        chunks = [(c // NCH, c % NCH) for c in range(B * NCH)]
        N = len(chunks)

        def store(e, c):
            b, r = chunks[c]
            q = c % 2
            e.dma_start(k.d["x1"][b, :, :, r * NP:(r + 1) * NP].rearrange("h p n -> p h n"), XO[:, q, :, :])\
                .then_inc(s_st[q], 16)

        with p.block() as blk:
            @blk.sync
            def _(e):
                for dst, src in ((WE[:, :, :], k.d["w_expT"].rearrange("(h p) o -> p h o", p=HM)), (BE[:, :], k.d["b_expT"]),
                                 (BD[:, :], k.d["b_dcnT"]), (WA[:, :, :], k.d["w_attnT"].rearrange("(h p) o -> p h o", p=HM)),
                                 (BA[:, :], k.d["b_attn"]), (ON[:, :], k.d["c_ones"][0:1, 0:HM])):
                    e.dma_start(dst, src).then_inc(s_w, 16)
                take(e, s_w, 96)
                for s in s_wr:
                    e.sem_inc(s, 1)
                for b in range(B):
                    if b:
                        take(e, s_fbf)
                    for i in range(4):
                        r0 = 1 + b * NT + i * QR
                        e.dma_start(FB[:, i * QR:(i + 1) * QR, :, :],
                                    k.d["fd"][r0:r0 + QR].rearrange("y c (h p) x -> p (y c h) x", p=HM))\
                            .then_inc(s_fb[i], 16)
                    for r in range(NCH):
                        c = b * NCH + r
                        q = c % 2
                        take(e, s_xf[q])
                        e.dma_start(XI[:, q, :, :], k.x_v[b, :, :, r * NP:(r + 1) * NP].rearrange("h p n -> p h n"))\
                            .then_inc(s_xi[q], 16)

            @blk.scalar
            def _(e):
                take(e, s_wr[0])
                for b in range(B):
                    take(e, s_lx)
                    e.activation(L[:, 4:6], L[:, 4:6], ACT.Exp).then_inc(s_ex, 1)
                    take(e, s_bb)
                    for r in range(NCH):
                        c = b * NCH + r
                        q = c % 2
                        for h in range(2):
                            e.activation(G0[:, q, h, :].rearrange("p (y x) -> p y x", x=128),
                                         FB[:, 3 * r:3 * r + 3, h, :], ACT.Identity,
                                         bias=BB[:, h:h + 1], scale=AT[:, 1:2]).then_inc(s_g0, 1)
                        if c >= 1:
                            take(e, s_xo)
                            store(e, c - 1)
                take(e, s_xo)
                store(e, N - 1)
                for q in range(2):
                    take(e, s_st[q], 16)

            @blk.tensor
            def _(e):
                take(e, s_wr[1])
                for b in range(B):
                    take(e, s_fa)
                    for h in range(2):
                        ins = e.matmul(PL[0:1, 0:2], FA[:, h:h + 1], WA[:, h, :], start=(h == 0), stop=(h == 1))
                    ins.then_inc(s_l, 1)
                    take(e, s_at)
                    e.matmul(PL[:, 4:6], ON[:, :], L[:, 4:6], start=True, stop=True).then_inc(s_ab, 1)
                    for r in range(NCH):
                        c = b * NCH + r
                        q = c % 2
                        take(e, s_g1)
                        for m in range(2):
                            for h in range(2):
                                ins = e.matmul(PE[q][:, m, 0:NP], WE[:, h, m * HC:(m + 1) * HC], G1[:, q, h, :],
                                               start=(h == 0), stop=(h == 1))
                        ins.then_inc(s_pe, 1)

            @blk.vector
            def _(e):
                def chained(ins):
                    ins.then_inc(s_v, 1)
                    take(e, s_v)

                take(e, s_wr[2])
                for q in range(2):
                    e.sem_inc(s_xf[q], 1)
                for b in range(B):
                    for i in range(4):
                        take(e, s_fb[i], 16)
                        e.tensor_reduce(SM[:, i, :],
                                        FB[:, i * QR:(i + 1) * QR, :, :].rearrange("p y c x -> p c y x"),
                                        AX.XY, ALU.add).then_inc(s_v, 1)
                    take(e, s_v, 4)
                    chained(e.tensor_reduce(MN[:, :], SM[:, :, :].rearrange("p i c -> p c i"), AX.X, ALU.add))
                    chained(e.scalar_tensor_tensor(out=MN[:, :], in0=MN[:, :], scalar=1.0 / HW, in1=BD[:, :],
                                                   op0=ALU.mult, op1=ALU.add))
                    e.tensor_tensor(FA[:, :], MN[:, 0:2], MN[:, 2:4], ALU.add).then_inc(s_fa, 1)
                    take(e, s_l)
                    chained(e.tensor_tensor(L[:, 0:2], PL[0:1, 0:2], BA[:, :], ALU.add))
                    chained(e.tensor_reduce(L[:, 2:3], L[:, 0:2], AX.X, ALU.max))
                    e.tensor_scalar(L[:, 4:6], L[:, 0:2], L[:, 2:3], None, ALU.subtract).then_inc(s_lx, 1)
                    take(e, s_ex)
                    chained(e.tensor_reduce(L[:, 2:3], L[:, 4:6], AX.X, ALU.add))
                    chained(e.reciprocal(L[:, 3:4], L[:, 2:3]))
                    e.tensor_scalar(L[:, 4:6], L[:, 4:6], L[:, 3:4], None, ALU.mult).then_inc(s_at, 1)
                    take(e, s_ab)
                    chained(e.tensor_copy(AT[:, :], PL[:, 4:6]))
                    chained(e.tensor_scalar(BB[:, :], BD[:, 0:2], AT[:, 1:2], None, ALU.mult))
                    e.scalar_tensor_tensor(out=BB[:, :], in0=BD[:, 2:4], scalar=AT[:, 0:1], in1=BB[:, :],
                                           op0=ALU.mult, op1=ALU.add).then_inc(s_bb, 1)

                    def expand(c):
                        q = c % 2
                        take(e, s_pe)
                        take(e, s_xi[q], 16)
                        if c >= 2:
                            take(e, s_st[q], 16)
                        for m in range(2):
                            e.scalar_tensor_tensor(out=XO[:, q, m, :], in0=PE[q][:, m, 0:NP], scalar=BE[:, m:m + 1],
                                                   in1=XI[:, q, m, :], op0=ALU.add, op1=ALU.add).then_inc(s_v, 1)
                        take(e, s_v, 2)
                        bb, r = chunks[c]
                        for m in range(2):
                            ins = e.bn_stats(k.ST[:, 2 * bb + m, r, :], XO[:, q, m, :])
                        ins.then_inc(s_xo, 1)
                        p.tick(e, s_xf[q])

                    for r in range(NCH):
                        c = b * NCH + r
                        q = c % 2
                        take(e, s_g0, 2)
                        for h in range(2):
                            ins = e.scalar_tensor_tensor(out=G1[:, q, h, :].rearrange("p (y x) -> p y x", x=128),
                                                         in0=FB[:, 3 * r:3 * r + 3, 2 + h, :], scalar=AT[:, 0:1],
                                                         in1=G0[:, q, h, :].rearrange("p (y x) -> p y x", x=128),
                                                         op0=ALU.mult, op1=ALU.add)
                        ins.then_inc(s_g1, 1)
                        if r >= 1:
                            expand(c - 1)
                    expand(b * NCH + NCH - 1)
                    if b + 1 < B:
                        p.tick(e, s_fbf)
                for q in range(2):
                    take(e, s_xf[q])


def edges_and_merge(nc, k):
    RC = 4
    NP = RC * W
    NCH = H // RC
    WP = W + 2
    with Phase(nc, "ed") as p:
        GN = p.sb([HC, 4, 2])
        group_norm_terms(nc, k, k.ST, NCH, GN)
        X1 = p.sb([HC, 2, HW])
        XP = p.sb([HC, 2, (H + 2) * WP])
        T1 = p.sb([HC, 2, 2, NP])
        T2 = p.sb([HC, 2, 2, NP])
        E = p.sb([HC, 2, 2, NP])
        XO = p.sb([HC, 2, 2, NP])
        WM = p.sb([HC, 2, C])
        BM = p.sb([HC, 2])
        PE = [p.ps([HC, 2, 512]) for _ in range(2)]
        s_w, s_v, s_z, s_xn, s_t, s_e, s_pe, s_xo, s_bf, s_tf, s_x1f = p.sems(11)
        s_wr = p.sems(2)
        s_x1 = p.sems(4)
        s_st = p.sems(2)
        QR = H // 4
        XPv = XP[:, :, :].rearrange("p h (y x) -> p h y x", x=WP)
        chunks = [(c // NCH, c % NCH) for c in range(B * NCH)]

        def at(r, dy, dx, h):
            return XPv[:, h, r * RC + 1 + dy:r * RC + 1 + dy + RC, 1 + dx:1 + dx + W]

        def tile(T, q, h):
            return T[:, q, h, :].rearrange("p (y x) -> p y x", x=W)

        with p.block() as blk:
            @blk.sync
            def _(e):
                e.dma_start(WM[:, :, :], k.d["w_mergeT"].rearrange("(h p) o -> p h o", p=HC)).then_inc(s_w, 16)
                e.dma_start(BM[:, :], k.d["b_mergeT"]).then_inc(s_w, 16)
                take(e, s_w, 32)
                for s in s_wr:
                    e.sem_inc(s, 1)
                for b in range(B):
                    if b:
                        take(e, s_x1f)
                    for i in range(4):
                        n0, n1 = i * QR * W, (i + 1) * QR * W
                        e.dma_start(X1[:, :, n0:n1], k.d["x1"][b, :, :, n0:n1].rearrange("h p n -> p h n"))\
                            .then_inc(s_x1[i], 16)
                    for r in range(NCH):
                        c = b * NCH + r
                        q = c % 2
                        take(e, s_xo)
                        e.dma_start(k.d["x2"][b, :, :, r * NP:(r + 1) * NP].rearrange("h p n -> p h n"), XO[:, q, :, :])\
                            .then_inc(s_st[q], 16)
                for q in range(2):
                    take(e, s_st[q], 16)

            @blk.scalar
            def _(e):
                take(e, s_z)
                for b in range(B):
                    if b:
                        take(e, s_bf)
                    for i in range(4):
                        take(e, s_x1[i], 16)
                        for h in range(2):
                            e.activation(XPv[:, h, 1 + i * QR:1 + (i + 1) * QR, 1:1 + W],
                                         X1[:, h, i * QR * W:(i + 1) * QR * W].rearrange("p (y x) -> p y x", x=W),
                                         ACT.Identity, bias=GN[:, 2 * b + h, 1:2],
                                         scale=GN[:, 2 * b + h, 0:1]).then_inc(s_xn, 1)

            @blk.gpsimd
            def _(e):
                e.memset(XP[:, :, :], 0.0).then_inc(s_z, 1)
                for c, (b, r) in enumerate(chunks):
                    q = c % 2
                    if r == 0:
                        take(e, s_xn, 2)
                    elif r % (NCH // 4) == NCH // 4 - 1 and r < NCH - 1:
                        take(e, s_xn, 2)
                    if c >= 2:
                        take(e, s_tf)
                    for h in range(2):
                        e.tensor_tensor(tile(T1, q, h), at(r, -1, 0, h), at(r, 1, 0, h), ALU.add)
                        ins = e.tensor_tensor(tile(T2, q, h), at(r, 0, -1, h), at(r, 0, 1, h), ALU.add)
                    ins.then_inc(s_t, 1)

            @blk.tensor
            def _(e):
                take(e, s_wr[0])
                for c in range(len(chunks)):
                    q = c % 2
                    take(e, s_e)
                    for m in range(2):
                        for h in range(2):
                            ins = e.matmul(PE[q][:, m, 0:NP], WM[:, h, m * HC:(m + 1) * HC], E[:, q, h, :],
                                           start=(h == 0), stop=(h == 1))
                    ins.then_inc(s_pe, 1)

            @blk.vector
            def _(e):
                take(e, s_wr[1])

                def merge(c):
                    b, r = chunks[c]
                    q = c % 2
                    take(e, s_pe)
                    if c >= 2:
                        take(e, s_st[q], 16)
                    for m in range(2):
                        e.scalar_tensor_tensor(out=XO[:, q, m, :], in0=PE[q][:, m, 0:NP], scalar=BM[:, m:m + 1],
                                               in1=X1[:, m, r * NP:(r + 1) * NP],
                                               op0=ALU.add, op1=ALU.add).then_inc(s_v, 1)
                    take(e, s_v, 2)
                    for m in range(2):
                        ins = e.bn_stats(k.ST[:, 2 * b + m, r, :], XO[:, q, m, :])
                    ins.then_inc(s_xo, 1)

                for c, (b, r) in enumerate(chunks):
                    q = c % 2
                    take(e, s_t)
                    for h in range(2):
                        e.tensor_tensor(T1[:, q, h, :], T1[:, q, h, :], T2[:, q, h, :], ALU.add).then_inc(s_v, 1)
                    take(e, s_v, 2)
                    for h in range(2):
                        ins = e.scalar_tensor_tensor(out=tile(E, q, h), in0=at(r, 0, 0, h), scalar=5.0,
                                                     in1=tile(T1, q, h), op0=ALU.mult, op1=ALU.subtract)
                    ins.then_inc(s_e, 1)
                    if c + 2 < len(chunks):
                        p.tick(e, s_tf)
                    if r == NCH - 1 and b + 1 < B:
                        p.tick(e, s_bf)
                    if r >= 1:
                        merge(c - 1)
                    if r == NCH - 1:
                        merge(c)
                        if b + 1 < B:
                            p.tick(e, s_x1f)


def wkv(nc, k):
    T = 512
    NCH = HW // T
    with Phase(nc, "wk") as p:
        GN = p.sb([HC, 4, 2])
        group_norm_terms(nc, k, k.ST, 24, GN)
        XI = p.sb([HC, 6, 2, T])
        XN = p.sb([HC, 2, 2, T])
        KT = p.sb([HC, 3, 2, T])
        VT = p.sb([HC, 3, 2, T])
        A2 = p.sb([HC, 2, 2, T])
        B2 = p.sb([HC, 2, 2, T])
        DP = p.sb([HC, 2, 2, T])
        AO = p.sb([HC, 2, 2, T])
        BO = p.sb([HC, 3, 2, T])
        B2V = p.sb([HC, 2, 2, T])
        BV = p.sb([HC, 2, 2, T])
        T1 = p.sb([HC, 2, 2, T])
        T3 = p.sb([HC, 2, 2, T])
        Y = p.sb([HC, 2, 2, T])
        S = p.sb([HC, 4, 3, 2, T + 1])
        WK = p.sb([HC, 2, C])
        WV = p.sb([HC, 2, C])
        WD = p.sb([HC, 2])
        U = p.sb([HC, 2])
        PK = [p.ps([HC, 2, T]) for _ in range(2)]
        PV = [p.ps([HC, 2, T]) for _ in range(2)]
        (s_w, s_v, s_va, s_xn, s_kv, s_k, s_o, s_ad, s_b2, s_e, s_p, s_y, s_bf, s_wd, s_t1, s_t3) = p.sems(16)
        s_wr = p.sems(3)
        s_xi = p.sems(6)
        s_st = p.sems(2)
        units = [(s, c) for c in range(NCH) for s in range(4)]
        N = len(units)

        def place(n):
            s, c = units[n]
            back = s % 2
            return s // 2, back, (NCH - 1 - c if back else c) * T

        with p.block() as blk:
            @blk.sync
            def _(e):
                for dst, src in ((WK[:, :, :], k.d["w_kT"].rearrange("(h p) o -> p h o", p=HC)),
                                 (WV[:, :, :], k.d["w_vT"].rearrange("(h p) o -> p h o", p=HC)),
                                 (WD[:, :], k.d["w_decayT"]), (U[:, :], k.d["uT"])):
                    e.dma_start(dst, src).then_inc(s_w, 16)
                take(e, s_w, 64)
                for s in s_wr:
                    e.sem_inc(s, 1)

                def load(n):
                    b, _b, t0 = place(n)
                    e.dma_start(XI[:, n % 6, :, :], k.d["x2"][b, :, :, t0:t0 + T].rearrange("h p n -> p h n"))\
                        .then_inc(s_xi[n % 6], 16)

                for n in range(5):
                    load(n)
                for n in range(N):
                    if n + 5 < N:
                        load(n + 5)
                    take(e, s_y)
                    b, back, t0 = place(n)
                    dst = k.d["ybd"] if back else k.d["yfd"]
                    e.dma_start(dst[b, :, :, t0:t0 + T].rearrange("h p n -> p h n"), Y[:, n % 2, :, :])\
                        .then_inc(s_st[n % 2], 16)
                for q in range(2):
                    take(e, s_st[q], 16)

            @blk.scalar
            def _(e):
                take(e, s_wr[0])
                e.activation(WD[:, :], WD[:, :], ACT.Exp).then_inc(s_wd, 1)

                def norm(n):
                    b, back, _t = place(n)
                    take(e, s_xi[n % 6], 16)
                    for h in range(2):
                        x = XI[:, n % 6, h, ::-1] if back else XI[:, n % 6, h, :]
                        ins = e.activation(XN[:, n % 2, h, :], x, ACT.Identity,
                                           bias=GN[:, 2 * b + h, 1:2], scale=GN[:, 2 * b + h, 0:1])
                    ins.then_inc(s_xn, 1)

                norm(0)
                for n in range(N):
                    q = n % 2
                    if n + 1 < N:
                        norm(n + 1)
                    if n >= 3:
                        take(e, s_bf)
                    take(e, s_kv)
                    e.activation(VT[:, n % 3, :, :], PV[q][:, :, :], ACT.Copy)
                    e.activation(KT[:, n % 3, :, :], PK[q][:, :, :], ACT.Copy).then_inc(s_k, 1)
                    take(e, s_ad)
                    e.activation(AO[:, q, :, :], DP[:, q, :, :], ACT.Relu).then_inc(s_va, 1)
                    e.activation(BO[:, n % 3, :, :], DP[:, q, :, :], ACT.Relu, scale=-1.0).then_inc(s_va, 1)
                    e.activation(A2[:, q, :, :], A2[:, q, :, :], ACT.Exp)
                    take(e, s_va, 2)
                    e.activation(AO[:, q, :, :], AO[:, q, :, :], ACT.Exp, scale=-1.0)
                    e.activation(BO[:, n % 3, :, :], BO[:, n % 3, :, :], ACT.Exp, scale=-1.0)
                    take(e, s_b2)
                    e.activation(B2[:, q, :, :], B2[:, q, :, :], ACT.Exp).then_inc(s_e, 1)
                take(e, s_bf, 3)

            @blk.tensor
            def _(e):
                take(e, s_wr[1])
                for n in range(N):
                    q = n % 2
                    take(e, s_xn)
                    for P_, W_ in ((PV[q], WV), (PK[q], WK)):
                        for m in range(2):
                            for h in range(2):
                                ins = e.matmul(P_[:, m, :], W_[:, h, m * HC:(m + 1) * HC], XN[:, q, h, :],
                                               start=(h == 0), stop=(h == 1))
                    ins.then_inc(s_kv, 1)

            @blk.gpsimd
            def _(e):
                def spread(n):
                    q = n % 2
                    take(e, s_o)
                    s = units[n][0]
                    e.tensor_tensor(B2[:, q, :, :], KT[:, n % 3, :, :], S[:, s, 0, :, 1:T + 1], ALU.subtract)\
                        .then_inc(s_b2, 1)

                def weigh(n):
                    q = n % 2
                    take(e, s_e)
                    e.tensor_tensor(B2V[:, q, :, :], B2[:, q, :, :], VT[:, n % 3, :, :], ALU.mult)
                    e.tensor_tensor(BV[:, q, :, :], BO[:, n % 3, :, :], VT[:, n % 3, :, :], ALU.mult).then_inc(s_p, 1)

                def add(n):
                    q = n % 2
                    take(e, s_t1)
                    e.tensor_tensor(T3[:, q, :, :], T3[:, q, :, :], BO[:, n % 3, :, :], ALU.add)
                    e.tensor_tensor(T1[:, q, :, :], T1[:, q, :, :], BV[:, q, :, :], ALU.add).then_inc(s_t3, 1)

                for n in range(N + 1):
                    if n >= 1:
                        weigh(n - 1)
                    if n < N:
                        spread(n)
                    if n >= 1:
                        add(n - 1)

            @blk.vector
            def _(e):
                take(e, s_wr[2])
                take(e, s_wd)
                e.tensor_scalar(WD[:, :], WD[:, :], -1.0, None, ALU.mult).then_inc(s_v, 1)
                e.memset(S[:, :, 0, :, T:T + 1], -1e38).then_inc(s_v, 1)
                e.memset(S[:, :, 1:3, :, T:T + 1], 0.0).then_inc(s_v, 1)
                take(e, s_v, 3)
                for q in range(2):
                    e.sem_inc(s_st[q], 16)

                def maxima(n):
                    q = n % 2
                    s = units[n][0]
                    take(e, s_k)
                    e.tensor_copy(S[:, s, :, :, 0:1], S[:, s, :, :, T:T + 1]).then_inc(s_v, 1)
                    take(e, s_v)
                    for m in range(2):
                        e.tensor_tensor_scan(S[:, s, 0, m, 1:T + 1], WD[:, m:m + 1].to_broadcast([HC, T]),
                                             KT[:, n % 3, m, :], S[:, s, 0, m, 0:1], ALU.add, ALU.max).then_inc(s_v, 1)
                    take(e, s_v, 2)
                    for m in range(2):
                        ins = e.scalar_tensor_tensor(out=DP[:, q, m, :], in0=KT[:, n % 3, m, :], scalar=U[:, m:m + 1],
                                                     in1=S[:, s, 0, m, 0:T], op0=ALU.add, op1=ALU.subtract)
                    ins.then_inc(s_o, 1)
                    for m in range(2):
                        ins = e.scalar_tensor_tensor(out=A2[:, q, m, :], in0=S[:, s, 0, m, 0:T],
                                                     scalar=WD[:, m:m + 1], in1=S[:, s, 0, m, 1:T + 1],
                                                     op0=ALU.add, op1=ALU.subtract)
                    ins.then_inc(s_ad, 1)

                def sums(n):
                    q = n % 2
                    s = units[n][0]
                    take(e, s_p)
                    p.tick(e, s_bf)
                    for i, D in ((1, B2V), (2, B2)):
                        for m in range(2):
                            e.tensor_tensor_scan(S[:, s, i, m, 1:T + 1], A2[:, q, m, :], D[:, q, m, :],
                                                 S[:, s, i, m, 0:1], ALU.mult, ALU.add).then_inc(s_v, 1)
                    take(e, s_v, 4)
                    e.tensor_tensor(T3[:, q, :, :], AO[:, q, :, :], S[:, s, 2, :, 0:T], ALU.mult)
                    e.tensor_tensor(T1[:, q, :, :], AO[:, q, :, :], S[:, s, 1, :, 0:T], ALU.mult).then_inc(s_t1, 1)

                def divide(n):
                    q = n % 2
                    take(e, s_t3)
                    e.reciprocal(T3[:, q, :, :], T3[:, q, :, :]).then_inc(s_v, 1)
                    take(e, s_v)
                    take(e, s_st[q], 16)
                    y = Y[:, q, :, ::-1] if place(n)[1] else Y[:, q, :, :]
                    e.tensor_tensor(y, T1[:, q, :, :], T3[:, q, :, :], ALU.mult).then_inc(s_y, 1)

                for n in range(N + 2):
                    if n < N:
                        maxima(n)
                    if n >= 2:
                        divide(n - 2)
                    if 1 <= n <= N:
                        sums(n - 1)


def gate_and_project(nc, k):
    T = 512
    NCH = HW // T
    R = 6
    with Phase(nc, "gp") as p:
        GN = p.sb([HC, 4, 2])
        group_norm_terms(nc, k, k.ST, 24, GN)
        XI = p.sb([HC, R, 2, T])
        YF = p.sb([HC, R, 2, T])
        YB = p.sb([HC, R, 2, T])
        XN = p.sb([HC, 2, 2, T])
        SG = p.sb([HC, 2, 2, T])
        HH = p.sb([HC, 3, 2, T])
        SQ = p.sb([HC, 2, 2, T])
        RS = p.sb([HC, 2, T])
        HN = p.sb([HC, 2, 2, T])
        XO = p.sb([HC, 2, 2, T])
        WR = p.sb([HC, 2, C])
        WO = p.sb([HC, 2, C])
        GB = p.sb([HC, 2, 2])
        AV = p.sb([HC, HC])
        PR = p.ps([HC, 2, T])
        PM = [p.ps([HC, T]) for _ in range(2)]
        PV = [p.ps([HC, T]) for _ in range(2)]
        PO = p.ps([HC, 2, T])
        (s_w, s_v, s_xn, s_r, s_sg, s_s, s_h, s_m, s_d, s_sq, s_var, s_ve, s_sd, s_hn, s_af, s_po, s_xo,
         s_pof) = p.sems(18)
        s_wr = p.sems(3)
        s_xi = p.sems(R)
        s_yy = p.sems(R)
        s_st = p.sems(2)
        N = B * NCH

        with p.block() as blk:
            @blk.sync
            def _(e):
                for dst, src in ((WR[:, :, :], k.d["w_rT"].rearrange("(h p) o -> p h o", p=HC)),
                                 (WO[:, :, :], k.d["w_oT"].rearrange("(h p) o -> p h o", p=HC)),
                                 (GB[:, :, :], k.d["ln_T"]), (AV[:, :], k.d["c_avg"])):
                    e.dma_start(dst, src).then_inc(s_w, 16)
                take(e, s_w, 64)
                for s in s_wr:
                    e.sem_inc(s, 1)

                def load(n):
                    b, t0 = n // NCH, n % NCH * T
                    i = n % R
                    e.dma_start(XI[:, i, :, :], k.d["x2"][b, :, :, t0:t0 + T].rearrange("h p n -> p h n"))\
                        .then_inc(s_xi[i], 16)
                    for Y_, src in ((YF, k.d["yfd"]), (YB, k.d["ybd"])):
                        e.dma_start(Y_[:, i, :, :], src[b, :, :, t0:t0 + T].rearrange("h p n -> p h n"))\
                            .then_inc(s_yy[i], 16)

                for n in range(5):
                    load(n)
                for n in range(N):
                    b, t0 = n // NCH, n % NCH * T
                    if n + 5 < N:
                        load(n + 5)
                    take(e, s_xo)
                    e.dma_start(k.d["x3"][b, :, :, t0:t0 + T].rearrange("h p n -> p h n"), XO[:, n % 2, :, :])\
                        .then_inc(s_st[n % 2], 16)
                for q in range(2):
                    take(e, s_st[q], 16)

            @blk.scalar
            def _(e):
                take(e, s_wr[0])

                def norm(n):
                    b = n // NCH
                    take(e, s_xi[n % R], 16)
                    for h in range(2):
                        ins = e.activation(XN[:, n % 2, h, :], XI[:, n % R, h, :], ACT.Identity,
                                           bias=GN[:, 2 * b + h, 1:2], scale=GN[:, 2 * b + h, 0:1])
                    ins.then_inc(s_xn, 1)

                norm(0)
                for n in range(N + 2):
                    if n < N:
                        take(e, s_r)
                        e.activation(SG[:, n % 2, :, :], PR[:, :, :], ACT.Sigmoid).then_inc(s_sg, 1)
                    if n + 1 < N:
                        norm(n + 1)
                    if 1 <= n <= N:
                        take(e, s_d)
                        e.activation(SQ[:, (n - 1) % 2, :, :], HH[:, (n - 1) % 3, :, :], ACT.Square).then_inc(s_sq, 1)
                    if n >= 2:
                        q = n % 2
                        take(e, s_ve)
                        e.activation(RS[:, q, :], RS[:, q, :], ACT.Sqrt).then_inc(s_sd, 1)
                        take(e, s_hn)
                        for h in range(2):
                            ins = e.activation(HN[:, q, h, :], HN[:, q, h, :], ACT.Identity,
                                               bias=GB[:, h, 1:2], scale=GB[:, h, 0:1])
                        ins.then_inc(s_af, 1)

            @blk.tensor
            def _(e):
                take(e, s_wr[1])

                def project(P_, W_, X_, sem):
                    for m in range(2):
                        for h in range(2):
                            ins = e.matmul(P_[:, m, :], W_[:, h, m * HC:(m + 1) * HC], X_[:, h, :],
                                           start=(h == 0), stop=(h == 1))
                    ins.then_inc(sem, 1)

                def average(P_, X_, sem):
                    for h in range(2):
                        ins = e.matmul(P_[:, :], AV[:, :], X_[:, h, :], start=(h == 0), stop=(h == 1))
                    ins.then_inc(sem, 1)

                take(e, s_xn)
                project(PR, WR, XN[:, 0], s_r)
                for n in range(N + 2):
                    if n < N:
                        take(e, s_h)
                        average(PM[n % 2], HH[:, n % 3], s_m)
                    if n + 1 < N:
                        take(e, s_xn)
                        project(PR, WR, XN[:, (n + 1) % 2], s_r)
                    if 1 <= n <= N:
                        take(e, s_sq)
                        average(PV[(n - 1) % 2], SQ[:, (n - 1) % 2], s_var)
                    if n >= 2:
                        take(e, s_af)
                        take(e, s_pof)
                        project(PO, WO, HN[:, n % 2], s_po)

            @blk.gpsimd
            def _(e):
                for n in range(N):
                    i = n % R
                    take(e, s_yy[i], 32)
                    e.tensor_tensor(YF[:, i, :, :], YF[:, i, :, :], YB[:, i, :, :], ALU.add).then_inc(s_s, 1)

            @blk.vector
            def _(e):
                take(e, s_wr[2])
                for q in range(2):
                    e.sem_inc(s_st[q], 16)
                e.sem_inc(s_pof, 1)
                for n in range(N + 3):
                    if n < N:
                        take(e, s_s)
                        take(e, s_sg)
                        e.scalar_tensor_tensor(out=HH[:, n % 3, :, :], in0=YF[:, n % R, :, :], scalar=0.5,
                                               in1=SG[:, n % 2, :, :], op0=ALU.mult, op1=ALU.mult).then_inc(s_h, 1)
                    if 1 <= n <= N:
                        i = (n - 1) % 3
                        take(e, s_m)
                        e.tensor_tensor(HH[:, i, :, :], HH[:, i, :, :],
                                        PM[(n - 1) % 2][:, :].unsqueeze(1).to_broadcast([HC, 2, T]),
                                        ALU.subtract).then_inc(s_d, 1)
                    if 2 <= n < N + 2:
                        take(e, s_var)
                        e.tensor_scalar(RS[:, n % 2, :], PV[n % 2][:, :], EPS, None, ALU.add).then_inc(s_ve, 1)
                    if n >= 3:
                        c, q = n - 3, (n - 3) % 2
                        take(e, s_po)
                        take(e, s_st[q], 16)
                        e.tensor_tensor(XO[:, q, :, :], PO[:, :, :], XI[:, c % R, :, :], ALU.add).then_inc(s_v, 1)
                        p.tick(e, s_pof)
                        take(e, s_v)
                        for m in range(2):
                            ins = e.bn_stats(k.ST2[:, 2 * (c // NCH) + m, c % NCH, :], XO[:, q, m, :])
                        ins.then_inc(s_xo, 1)
                    if 2 <= n < N + 2:
                        q, i = n % 2, (n - 2) % 3
                        take(e, s_sd)
                        e.reciprocal(RS[:, q, :], RS[:, q, :]).then_inc(s_v, 1)
                        take(e, s_v)
                        e.tensor_tensor(HN[:, q, :, :], HH[:, i, :, :],
                                        RS[:, q, :].unsqueeze(1).to_broadcast([HC, 2, T]),
                                        ALU.mult).then_inc(s_hn, 1)
                take(e, s_pof)


DI = 2 * C
ND = DI // 128
RK = 12
NS = 16


def mamba_inputs(nc, k):
    T = 512
    NCH = HW // T
    with Phase(nc, "mi") as p:
        GN = p.sb([HC, 4, 2])
        group_norm_terms(nc, k, k.ST2, 18, GN)
        XI = p.sb([HC, 3, 2, T])
        XN = p.sb([HC, 3, 2, T])
        XH = p.sb([128, 2, ND, T + 3])
        CV = p.sb([128, 2, ND, T])
        XV = p.sb([128, 2, ND, T])
        SZ = p.sb([128, 2, ND, T])
        XD = p.sb([RK + 2 * NS, 2, T])
        XS = p.sb([128, 2, ND, T])
        EE = p.sb([128, 2, ND, T])
        DL = p.sb([128, 2, ND, T])
        PP = p.sb([128, 2, ND, T])
        PM = p.sb([128, 2, ND, T])
        WI = p.sb([HC, 2, 2 * DI])
        WX = p.sb([128, ND, RK + 2 * NS])
        WT = p.sb([RK, DI])
        CW = p.sb([128, ND, 4])
        CB = p.sb([128, ND])
        BT = p.sb([128, ND])
        PX = p.ps([128, ND, T])
        PZ = p.ps([128, ND, T])
        PD = p.ps([RK + 2 * NS, T])
        (s_w, s_v, s_va, s_p, s_xn, s_px, s_pz, s_xh, s_cv, s_xv, s_zf, s_pd, s_xd, s_sx, s_dt, s_df, s_ex,
         s_ln, s_pp, s_so, s_fe, s_b2) = p.sems(22)
        s_wr = p.sems(3)
        s_xi = p.sems(3)
        s_sxv, s_ssz, s_sxd, s_sdl = (p.sems(2) for _ in range(4))
        N = B * NCH

        def flat(t, q):
            return t[:, q, :, :].rearrange("p d t -> p (d t)")

        def cols(dram, n):
            b, t0 = n // NCH, n % NCH * T
            return dram[b, :, t0:t0 + T].rearrange("(d p) t -> p d t", p=128)

        with p.block() as blk:
            @blk.sync
            def _(e):
                for dst, src in ((WI[:, :, :], k.d["w_inT"].rearrange("(h p) o -> p h o", p=HC)),
                                 (WX[:, :, :], k.d["w_xT"].rearrange("(d p) o -> p d o", p=128)),
                                 (WT[:, :], k.d["w_dtT"]), (CW[:, :, :], k.d["conv_wT"]),
                                 (CB[:, :], k.d["conv_bT"]), (BT[:, :], k.d["b_dtT"])):
                    e.dma_start(dst, src).then_inc(s_w, 16)
                take(e, s_w, 96)
                for s in s_wr:
                    e.sem_inc(s, 1)

                def load(n):
                    b, t0 = n // NCH, n % NCH * T
                    e.dma_start(XI[:, n % 3, :, :], k.d["x3"][b, :, :, t0:t0 + T].rearrange("h p n -> p h n"))\
                        .then_inc(s_xi[n % 3], 16)

                for n in range(3):
                    load(n)
                for n in range(N + 2):
                    q = n % 2
                    if n >= 2:
                        take(e, s_so)
                        e.dma_start(cols(k.d["dld"], n - 2), DL[:, q, :, :]).then_inc(s_sdl[q], 16)
                    if n < N:
                        take(e, s_sx)
                        b, t0 = n // NCH, n % NCH * T
                        e.dma_start(cols(k.d["xvd"], n), XV[:, q, :, :]).then_inc(s_sxv[q], 16)
                        e.dma_start(k.d["bcd"][b, :, t0:t0 + T], XD[RK:, q, :]).then_inc(s_sxd[q], 16)
                    m = n - 1 if n < N else n - 2
                    if 0 <= m and n != N:
                        e.dma_start(cols(k.d["szd"], m), SZ[:, m % 2, :, :]).then_inc(s_ssz[m % 2], 16)
                    if n + 3 < N:
                        load(n + 3)

            @blk.scalar
            def _(e):
                take(e, s_wr[0])
                for q in range(2):
                    e.sem_inc(s_ssz[q], 16)
                    e.sem_inc(s_sxv[q], 16)
                    e.sem_inc(s_sdl[q], 16)

                def norm(n):
                    b = n // NCH
                    take(e, s_xi[n % 3], 16)
                    for h in range(2):
                        ins = e.activation(XN[:, n % 3, h, :], XI[:, n % 3, h, :], ACT.Identity,
                                           bias=GN[:, 2 * b + h, 1:2], scale=GN[:, 2 * b + h, 0:1])
                    ins.then_inc(s_xn, 1)

                def fill(n):
                    take(e, s_px)
                    e.activation(XH[:, n % 2, :, 3:T + 3], PX[:, :, :], ACT.Copy).then_inc(s_xh, 1)

                norm(0)
                fill(0)
                norm(1)
                take(e, s_b2)
                for n in range(N + 1):
                    q, r = n % 2, (n - 1) % 2
                    if n >= 1:
                        take(e, s_pz)
                        take(e, s_ssz[r], 16)
                        e.activation(SZ[:, r, :, :], PZ[:, :, :], ACT.Silu).then_inc(s_zf, 1)
                    if n < N:
                        take(e, s_cv)
                        take(e, s_sxv[q], 16)
                        e.activation(XV[:, q, :, :], CV[:, q, :, :], ACT.Silu).then_inc(s_xv, 1)
                    if n + 1 < N:
                        fill(n + 1)
                    if n >= 1:
                        take(e, s_dt)
                        take(e, s_fe)
                        for d in range(ND):
                            e.activation(XS[:, r, d, :], PZ[:, d, :], ACT.Relu, bias=BT[:, d:d + 1])
                        for d in range(ND):
                            ins = e.activation(EE[:, r, d, :], PZ[:, d, :], ACT.Abs, bias=BT[:, d:d + 1])
                        ins.then_inc(s_va, 1)
                        take(e, s_va)
                        e.sem_inc(s_df, 1)
                        e.activation(EE[:, r, :, :], EE[:, r, :, :], ACT.Exp, scale=-1.0).then_inc(s_va, 1)
                        take(e, s_va)
                        e.sem_inc(s_ex, 1)
                    if n + 2 < N:
                        norm(n + 2)
                    if n >= 1:
                        take(e, s_sdl[r], 16)
                        e.activation(DL[:, r, :, :], EE[:, r, :, :], ACT.Ln, bias=1.0).then_inc(s_ln, 1)
                for q in range(2):
                    take(e, s_ssz[q], 16)
                    take(e, s_sxv[q], 16)
                    take(e, s_sdl[q], 16)

            @blk.tensor
            def _(e):
                take(e, s_wr[1])

                def inner(n, P_, first, sem):
                    for d in range(ND):
                        for h in range(2):
                            o = first + d * 128
                            ins = e.matmul(P_[:, d, :], WI[:, h, o:o + 128], XN[:, n % 3, h, :],
                                           start=(h == 0), stop=(h == 1))
                    ins.then_inc(sem, 1)

                take(e, s_xn)
                inner(0, PX, 0, s_px)
                for n in range(N + 1):
                    if n + 1 < N:
                        take(e, s_xn)
                        inner(n + 1, PX, 0, s_px)
                    if n >= 1:
                        take(e, s_xd)
                        take(e, s_zf)
                        for d in range(ND):
                            ins = e.matmul(PZ[:, d, :], WT[:, d * 128:(d + 1) * 128], XD[0:RK, (n - 1) % 2, :],
                                           start=True, stop=True)
                        ins.then_inc(s_dt, 1)
                    if n < N:
                        take(e, s_xv)
                        for d in range(ND):
                            ins = e.matmul(PD[:, :], WX[:, d, :], XV[:, n % 2, d, :], start=(d == 0),
                                           stop=(d == ND - 1))
                        ins.then_inc(s_pd, 1)
                    if n >= 1:
                        take(e, s_df)
                    if n < N:
                        inner(n, PZ, DI, s_pz)

            @blk.gpsimd
            def _(e):
                for n in range(N):
                    q = n % 2
                    take(e, s_ex)
                    e.tensor_scalar(PP[:, q, :, :], EE[:, q, :, :], 1.0 / 3.0, -0.5, ALU.mult, ALU.add)\
                        .then_inc(s_p, 1)
                    e.tensor_scalar(PM[:, q, :, :], EE[:, q, :, :], NEAR1, None, ALU.is_le).then_inc(s_p, 1)
                    take(e, s_p, 2)
                    e.tensor_tensor(PP[:, q, :, :], PP[:, q, :, :], EE[:, q, :, :], ALU.mult)
                    e.tensor_tensor(PM[:, q, :, :], PM[:, q, :, :], EE[:, q, :, :], ALU.mult).then_inc(s_pp, 1)

            @blk.vector
            def _(e):
                take(e, s_wr[2])
                e.tensor_tensor(BT[:, :], BT[:, :], BT[:, :], ALU.add).then_inc(s_b2, 1)
                e.memset(XH[:, 1, :, T:T + 3], 0.0).then_inc(s_v, 1)
                take(e, s_v)
                for q in range(2):
                    e.sem_inc(s_sxd[q], 16)
                e.sem_inc(s_fe, 2)

                def conv(n):
                    q = n % 2
                    if n % NCH == 0 and n:
                        e.memset(XH[:, q, :, 0:3], 0.0).then_inc(s_v, 1)
                    else:
                        e.tensor_copy(XH[:, q, :, 0:3], XH[:, 1 - q, :, T:T + 3]).then_inc(s_v, 1)
                    take(e, s_xh)
                    take(e, s_v)
                    for d in range(ND):
                        e.tensor_scalar(CV[:, q, d, :], XH[:, q, d, 3:3 + T], CW[:, d, 3:4], CB[:, d:d + 1],
                                        ALU.mult, ALU.add).then_inc(s_v, 1)
                    for j in range(3):
                        take(e, s_v, 3)
                        for d in range(ND):
                            ins = e.scalar_tensor_tensor(out=CV[:, q, d, :], in0=XH[:, q, d, j:j + T],
                                                         scalar=CW[:, d, j:j + 1], in1=CV[:, q, d, :],
                                                         op0=ALU.mult, op1=ALU.add)
                            if j < 2:
                                ins.then_inc(s_v, 1)
                    ins.then_inc(s_cv, 1)

                def blend(q):
                    take(e, s_ln)
                    take(e, s_pp)
                    e.scalar_tensor_tensor(out=flat(DL, q), in0=flat(EE, q), scalar=NEAR1, in1=flat(DL, q),
                                           op0=ALU.is_gt, op1=ALU.mult).then_inc(s_v, 1)
                    e.scalar_tensor_tensor(out=flat(PP, q), in0=flat(PP, q), scalar=1.0, in1=flat(PM, q),
                                           op0=ALU.add, op1=ALU.mult).then_inc(s_v, 1)
                    take(e, s_v)
                    e.tensor_tensor(DL[:, q, :, :], DL[:, q, :, :], XS[:, q, :, :], ALU.add).then_inc(s_v, 1)
                    take(e, s_v, 2)
                    e.tensor_tensor(DL[:, q, :, :], DL[:, q, :, :], PP[:, q, :, :], ALU.add).then_inc(s_so, 1)
                    p.tick(e, s_fe)

                conv(0)
                for n in range(N + 2):
                    q = n % 2
                    if n >= 2:
                        blend(q)
                    if n + 1 < N:
                        conv(n + 1)
                    if n < N:
                        take(e, s_sxd[q], 16)
                        take(e, s_pd)
                        e.tensor_copy(XD[:, q, :], PD[:, :]).then_inc(s_xd, 1)
                        p.tick(e, s_sx)
                take(e, s_fe, 2)
                for q in range(2):
                    take(e, s_sxd[q], 16)


def mamba_scan(nc, k):
    T = 512
    NCH = HW // T
    NC = B * NCH
    N = NC * NS
    RB, RA, RG = 6, 3, 3
    with Phase(nc, "ms") as p:
        XV = p.sb([128, 2, ND, T])
        DL = p.sb([128, 2, ND, T])
        SZ = p.sb([128, 2, ND, T])
        DU = p.sb([128, 2, ND, T])
        XI = p.sb([HC, 2, 2, T])
        BC = p.sb([128, RB, 2, T])
        DB = p.sb([128, RB, ND, T])
        DA = p.sb([128, RA, ND, T])
        HH = p.sb([128, 3, ND, T])
        G = p.sb([128, RG, ND, T])
        YY = p.sb([128, ND, T])
        XO = p.sb([HC, 2, 2, T])
        TKP = p.sb([128, 1])
        CAR = p.sb([128, NS, ND])
        AL = p.sb([128, ND, NS])
        DD = p.sb([128, ND])
        WO = p.sb([128, ND, C])
        PY = [p.ps([128, ND, T]) for _ in range(2)]
        PO = p.ps([HC, 2, T])
        (s_w, s_v, s_c, s_al, s_da, s_bu, s_g, s_ra, s_rb, s_rg, s_yz, s_po, s_xo, s_y1, s_du, s_dp) = p.sems(16)
        s_wr = p.sems(3)
        s_bc = p.sems(RB)
        s_in = p.sems(2)
        s_st = p.sems(2)

        with p.block() as blk:
            @blk.sync
            def _(e):
                for dst, src in ((AL[:, :, :], k.d["a_log"].rearrange("(d p) n -> p d n", p=128)), (DD[:, :], k.d["d_T"]),
                                 (WO[:, :, :], k.d["w_outT"].rearrange("(d p) o -> p d o", p=128))):
                    e.dma_start(dst, src).then_inc(s_w, 16)
                take(e, s_w, 48)
                for s in s_wr:
                    e.sem_inc(s, 1)

                def load(c):
                    b, t0, q = c // NCH, c % NCH * T, c % 2
                    for dst, src in ((DL, k.d["dld"]), (XV, k.d["xvd"]), (SZ, k.d["szd"])):
                        e.dma_start(dst[:, q, :, :], src[b, :, t0:t0 + T].rearrange("(d p) t -> p d t", p=128))\
                            .then_inc(s_in[q], 16)
                    e.dma_start(XI[:, q, :, :], k.d["x3"][b, :, :, t0:t0 + T].rearrange("h p n -> p h n"))\
                        .then_inc(s_in[q], 16)

                def spread(i):
                    c, n = i // NS, i % NS
                    b, t0 = c // NCH, c % NCH * T
                    if i >= RB:
                        take(e, s_rb)
                    src = k.d["bcd"][b, n:n + NS + 1:NS, t0:t0 + T]
                    e.dma_start(BC[:, i % RB, :, :], src.unsqueeze(0).to_broadcast([128, 2, T]))\
                        .then_inc(s_bc[i % RB], 16)

                load(0)
                load(1)
                for i in range(N + 2 * NS):
                    if i < N:
                        spread(i)
                    c, n = i // NS - 1, i % NS
                    if n == 13 and 0 <= c < NC:
                        b, t0 = c // NCH, c % NCH * T
                        take(e, s_xo)
                        e.dma_start(k.out_v[b, :, :, t0:t0 + T].rearrange("h p n -> p h n"), XO[:, c % 2, :, :])\
                            .then_inc(s_st[c % 2], 16)
                        if c + 2 < NC:
                            load(c + 2)
                for q in range(2):
                    take(e, s_st[q], 16)
                take(e, s_rb, RB)

            @blk.scalar
            def _(e):
                take(e, s_wr[0])
                e.activation(AL[:, :, :], AL[:, :, :], ACT.Exp).then_inc(s_al, 1)
                take(e, s_y1)
                for i in range(N):
                    c, n = i // NS, i % NS
                    if n == 0:
                        take(e, s_du)
                    if i >= RA:
                        take(e, s_ra)
                    for d in range(ND):
                        ins = e.activation(DA[:, i % RA, d, :], DL[:, c % 2, d, :], ACT.Exp, scale=AL[:, d, n:n + 1])
                    ins.then_inc(s_da, 1)
                take(e, s_ra, RA)

            @blk.gpsimd
            def _(e):
                def gain(c):
                    q = c % 2
                    take(e, s_in[q], 64)
                    e.tensor_tensor(DU[:, q, :, :], DL[:, q, :, :], XV[:, q, :, :], ALU.mult).then_inc(s_du, 1)
                    e.tensor_tensor(TKP[:, :], TKP[:, :], TKP[:, :], ALU.mult).then_inc(s_dp, 1)
                    take(e, s_dp)

                e.memset(TKP[:, :], 0.0).then_inc(s_dp, 1)
                take(e, s_dp)
                gain(0)
                for i in range(N):
                    c, n = i // NS, i % NS
                    if n == 15 and c + 1 < NC:
                        gain(c + 1)
                    take(e, s_bc[i % RB], 16)
                    e.tensor_tensor(DB[:, i % RB, :, :], DU[:, c % 2, :, :],
                                    BC[:, i % RB, 0, :].unsqueeze(1).to_broadcast([128, ND, T]),
                                    ALU.mult).then_inc(s_bu, 1)

            @blk.tensor
            def _(e):
                take(e, s_wr[1])
                for i in range(N + NS):
                    c, n = i // NS, i % NS
                    if i < N:
                        take(e, s_g)
                        for d, sem in enumerate((s_ra, s_rb, s_rg)):
                            e.matmul(PY[c % 2][:, d, :], k.ident[:, :], G[:, i % RG, d, :], start=(n == 0),
                                     stop=(n == NS - 1)).then_inc(sem, 1)
                    if n == 5 and c >= 1:
                        take(e, s_yz)
                        for m in range(2):
                            for d in range(ND):
                                ins = e.matmul(PO[:, m, :], WO[:, d, m * HC:(m + 1) * HC], YY[:, d, :],
                                               start=(d == 0), stop=(d == ND - 1))
                        ins.then_inc(s_po, 1)

            @blk.vector
            def _(e):
                take(e, s_wr[2])
                take(e, s_al)
                e.tensor_scalar(AL[:, :, :], AL[:, :, :], -1.0, None, ALU.mult).then_inc(s_y1, 1)
                for q in range(2):
                    e.sem_inc(s_st[q], 16)
                e.sem_inc(s_rg, RG)
                e.memset(CAR[:, :, :], 0.0).then_inc(s_c, 1)

                def scan(i):
                    c, n = i // NS, i % NS
                    take(e, s_c)
                    take(e, s_bu)
                    take(e, s_da)
                    for d in range(ND):
                        e.tensor_tensor_scan(HH[:, i % 3, d, :], DA[:, i % RA, d, :], DB[:, i % RB, d, :],
                                             CAR[:, n, d:d + 1], ALU.mult, ALU.add).then_inc(s_v, 1)
                    take(e, s_v, ND)
                    if c % NCH == NCH - 1:
                        e.memset(CAR[:, n, :], 0.0).then_inc(s_c, 1)
                    else:
                        e.tensor_copy(CAR[:, n, :], HH[:, i % 3, :, T - 1]).then_inc(s_c, 1)

                def read(i):
                    take(e, s_rg)
                    e.tensor_tensor(G[:, i % RG, :, :], HH[:, i % 3, :, :],
                                    BC[:, i % RB, 1, :].unsqueeze(1).to_broadcast([128, ND, T]),
                                    ALU.mult).then_inc(s_g, 1)

                def finish(c):
                    q = c % 2
                    for d in range(ND):
                        e.scalar_tensor_tensor(out=YY[:, d, :], in0=XV[:, q, d, :], scalar=DD[:, d:d + 1],
                                               in1=PY[q][:, d, :], op0=ALU.mult, op1=ALU.add).then_inc(s_v, 1)
                    take(e, s_v, ND)
                    e.tensor_tensor(YY[:, :, :], YY[:, :, :], SZ[:, q, :, :], ALU.mult).then_inc(s_yz, 1)

                def put(c):
                    q = c % 2
                    take(e, s_po)
                    take(e, s_st[q], 16)
                    e.tensor_tensor(XO[:, q, :, :], PO[:, :, :], XI[:, q, :, :], ALU.add).then_inc(s_xo, 1)

                for i in range(N + NS):
                    c, n = i // NS, i % NS
                    if i < N:
                        scan(i)
                    if 1 <= i <= N:
                        read(i - 1)
                    if n == 3 and c >= 1:
                        if c == NC:
                            take(e, s_rg, RG)
                        finish(c - 1)
                    if n == 9 and c >= 1:
                        put(c - 1)
                take(e, s_c)


PHASES = (first_norm_and_projections, sample_and_convolve, mix_and_expand, edges_and_merge,
          wkv, gate_and_project, mamba_inputs, mamba_scan)


def program(nc, ins, out, phases=PHASES, kind="Internal"):
    k = Shared(ins)
    k.x_v = k.d["x"].rearrange("b (h p) y x -> b h p (y x)", p=HC)
    k.out_v = out.rearrange("b (h p) y x -> b h p (y x)", p=HC)
    scratch = {"xrT": [B, ROWS, W, CM], "sxd": [B, NT, 2, HM, 128], "oyd": [B, H, W, CM],
               "fd": [B * NT + 3, 2, CM, 128], "x1": [B, 2, HC, HW], "x2": [B, 2, HC, HW], "x3": [B, 2, HC, HW],
               "yfd": [B, 2, HC, HW], "ybd": [B, 2, HC, HW],
               "xvd": [B, DI, HW], "dld": [B, DI, HW], "szd": [B, DI, HW], "bcd": [B, 2 * NS, HW]}
    for n, shape in scratch.items():
        if n not in ins:
            k.d[n] = nc.dram_tensor(n, shape, F32, kind=kind).ap()
    k.oyd_v = k.d["oyd"].rearrange("b y x c -> b (y x) c").rearrange("b (t p) c -> b t p c", p=128)
    with Phase(nc, "top") as p:
        k.ident = p.sb([128, 128])
        k.G6 = p.sb([HC, HC])
        k.FLAG = p.sb([1, 4], I32)
        k.ST = p.sb([HC, 4, 24, 6])
        k.ST2 = p.sb([HC, 4, 18, 6])
        k.const_loads = [(k.ident[:, :], k.d["c_ident"]), (k.G6[:, :], k.d["c_g6"])]
        load_constants(nc, k)
        for phase in phases:
            phase(nc, k)


def layout(inp):
    f = np.float32
    d = {"x": inp["x"]}
    d["w_reduceT"] = inp["L0_conv_w_reduce"].T
    d["b_reduceT"] = inp["L0_conv_b_reduce"].reshape(2, HM).T
    wo = inp["L0_conv_w_offset"].reshape(2, HM, 2, CM).transpose(3, 2, 0, 1)[:, ::-1]
    d["w_offT"] = wo.reshape(CM, 4, HM)
    d["b_offT"] = inp["L0_conv_b_offset"].reshape(2, HM, 2).transpose(1, 2, 0)[:, ::-1].reshape(HM, 4)
    wd = np.stack([inp["L0_conv_w_dcnw"], inp["L0_conv_w_dcnh"]]).reshape(2, CM, NG, CG, TAPS)
    wd = wd.transpose(2, 4, 3, 0, 1).reshape(NG * TAPS * CG, 2, CM)
    wdp = np.zeros((NCK * 128, 2, CM), f)
    wdp[:len(wd)] = wd
    d["w_dcn"] = wdp.reshape(NCK, 128, 2, CM).transpose(1, 0, 2, 3)
    d["w_expT"] = inp["L0_conv_w_expand"].T
    d["b_expT"] = inp["L0_conv_b_expand"].reshape(2, HC).T
    d["b_dcnT"] = np.stack([inp["L0_conv_b_dcnw"], inp["L0_conv_b_dcnh"]]).reshape(4, HM).T
    d["w_attnT"] = inp["L0_conv_w_attn"].T
    d["b_attn"] = inp["L0_conv_b_attn"][None, :]
    d["w_mergeT"] = inp["L1_conv_merge_w"].reshape(C, C).T
    d["b_mergeT"] = inp["L1_conv_merge_b"].reshape(2, HC).T
    for n in "kvro":
        d[f"w_{n}T"] = inp["L2_conv_W" + n].T
    d["w_decayT"] = inp["L2_conv_w_decay"].reshape(2, HC).T
    d["uT"] = inp["L2_conv_u"].reshape(2, HC).T
    d["ln_T"] = np.stack([inp["L2_conv_ln_g"], inp["L2_conv_ln_b"]]).reshape(2, 2, HC).transpose(2, 1, 0)
    d["c_avg"] = np.full((HC, HC), 1.0 / C, f)
    d["w_inT"] = inp["L3_conv_W_in"].T
    d["conv_wT"] = inp["L3_conv_conv_w"].reshape(ND, 128, 4).transpose(1, 0, 2)
    d["conv_bT"] = inp["L3_conv_conv_b"].reshape(ND, 128).T
    d["w_xT"] = inp["L3_conv_W_x"].T
    d["w_dtT"] = inp["L3_conv_W_dt"].T
    d["b_dtT"] = inp["L3_conv_b_dt"].reshape(ND, 128).T
    d["a_log"] = inp["L3_conv_A_log"]
    d["d_T"] = inp["L3_conv_D"].reshape(ND, 128).T
    d["w_outT"] = inp["L3_conv_W_out"].T
    d["c_ones"] = np.ones((1, 128), f)
    d["c_ident"] = np.eye(128, dtype=f)
    i = np.arange(HC) // 6
    d["c_g6"] = (i[:, None] == i[None, :]).astype(f) / f(6)
    d["c_kx"] = ((np.arange(HM) % TAPS % 3) - 1).astype(f)[:, None]
    d["c_pxr"] = np.tile(np.arange(W, dtype=f), (HM, 4))
    d["c_qx"] = -np.arange(W, dtype=f)[:, None]
    px = np.arange(HW).reshape(NT, 1, 128, 1)
    y, y0 = px // W, px[:, :, :1] // W
    w, r = np.arange(NWIN).reshape(1, NWIN, 1, 1), np.arange(WIN)
    tab = np.zeros((2, NT, NWIN, 128, WIN + 1), f)
    tab[0, ..., :WIN] = y - y0 + 3 - r
    tab[1, ..., :WIN] = y - WIN * w + 1 - r
    tab[1, :, 1:, :, WIN] = 1
    d["c_tab"] = tab.reshape(-1, 128, WIN + 1)
    return {n: np.ascontiguousarray(np.asarray(a)) for n, a in d.items()}


def kernel(**inputs):
    import concourse.bacc as bacc
    from concourse.bass_utils import run_bass_kernel_spmd

    nc = bacc.Bacc("TRN2", target_bir_lowering=False, num_devices=1)
    arrays = layout({n: np.asarray(a) for n, a in inputs.items()})
    ins = {n: nc.dram_tensor(n, a.shape, mybir.dt.from_np(a.dtype), kind="ExternalInput").ap()
           for n, a in arrays.items()}
    out = nc.dram_tensor("out", [B, C, H, W], F32, kind="ExternalOutput").ap()
    program(nc, ins, out)
    r = run_bass_kernel_spmd(nc, [arrays], core_ids=[0])
    return r.results[0]["out"]
```
